# Optimizing a Trainium2 kernel written in Bass

```python
import numpy as np
import jax
import jax.numpy as jnp

def _softmax(x, axis=-1):
    return jax.nn.softmax(x, axis=axis)

def _gelu(x):
    return jax.nn.gelu(x, approximate=True)

def _silu(x):
    return jax.nn.silu(x)

def _sigmoid(x):
    return jax.nn.sigmoid(x)

def _layernorm(x, axis=-1, eps=1e-05):
    m = jnp.mean(x, axis=axis, keepdims=True)
    v = jnp.var(x, axis=axis, keepdims=True)
    return (x - m) / jnp.sqrt(v + eps)

def _scatter_add(tgt, idx, src, axis=0):
    return tgt.at[idx].add(src)

def _segment_sum(src, seg, n):
    return jax.ops.segment_sum(src, seg, n)
kernel_name = 'mk_xattn_ffn_d1_seqx_r2_eb90f3'

def setup_inputs(seed: int=0):
    np.random.seed(seed)
    _w = jnp.asarray

    def _rec_inputs():
        import jax
        import jax.numpy as jnp
        _rk = jax.random.key(seed)
        x = -0.0002928 + 1 * jax.random.normal(jax.random.fold_in(_rk, 1), (4, 2048, 512), jnp.float32)
        _lenS = 2048 - jax.random.randint(jax.random.fold_in(_rk, 7), (4,), 0, max(1, 2048 // 4) + 1, jnp.int32)
        _lenS2 = 128 - jax.random.randint(jax.random.fold_in(_rk, 8), (4,), 0, max(1, 128 // 4) + 1, jnp.int32)
        _ctx_1024P = jax.random.normal(jax.random.fold_in(_rk, 11), (4, 16, 512), jnp.float32)
        _ctx_1024c = jax.random.dirichlet(jax.random.fold_in(_rk, 511), 0.3 * jnp.ones((16,), jnp.float32), (4, 128))
        _ctx_1024t = jnp.einsum('bsk,bkd->bsd', _ctx_1024c, _ctx_1024P)
        _ctx_1024t = _ctx_1024t * jax.lax.rsqrt(jnp.mean(jnp.square(_ctx_1024t)) + 1e-12) * 0.953939
        ctx_1024 = -1.39393e-06 + 0.999914 * (_ctx_1024t + 0.3 * jax.random.normal(jax.random.fold_in(_rk, 611), (4, 128, 512), jnp.float32))
        return (x, ctx_1024)
    x, ctx_1024 = _rec_inputs()

    def _L0_xattn_setup():
        import jax, jax.numpy as jnp
        import numpy as np
        EMBED_DIM = 512
        NUM_HEADS = 16
        HEAD_DIM = EMBED_DIM // NUM_HEADS
        B, T, S = (2, 1024, 1024)
        key = jax.random.key(seed)
        ks = jax.random.split(key, 5)
        scale_w = 1.0 / np.sqrt(EMBED_DIM)
        return {'q': jax.random.normal(ks[0], (B, T, EMBED_DIM), dtype=jnp.float32), 'k': jax.random.normal(ks[1], (B, S, EMBED_DIM), dtype=jnp.float32), 'v': jax.random.normal(ks[2], (B, S, EMBED_DIM), dtype=jnp.float32), 'in_proj_weight': jax.random.normal(ks[3], (3 * EMBED_DIM, EMBED_DIM), dtype=jnp.float32) * scale_w, 'in_proj_bias': jnp.zeros((3 * EMBED_DIM,), dtype=jnp.float32), 'out_w': jax.random.normal(ks[4], (EMBED_DIM, EMBED_DIM), dtype=jnp.float32) * scale_w, 'out_b': jnp.zeros((EMBED_DIM,), dtype=jnp.float32)}
    _L0_xattn_all = _L0_xattn_setup()
    _L0_xattn_in = {k: v for k, v in _L0_xattn_all.items() if k in ('in_proj_weight', 'in_proj_bias', 'out_w', 'out_b')}
    del _L0_xattn_all

    def _L0_ffn_setup():
        import jax, jax.numpy as jnp
        import numpy as np
        D_MODEL = 512
        key = jax.random.key(seed)
        k_x, k_w, k_a1, k_a2 = jax.random.split(key, 4)
        x = jax.random.normal(k_x, (4, 1024, D_MODEL), dtype=jnp.float32)
        weight = jax.random.normal(k_w, (D_MODEL, D_MODEL), dtype=jnp.float32) * 0.02
        aux_weight1 = jax.random.normal(k_a1, (D_MODEL, D_MODEL), dtype=jnp.float32) * 0.02
        aux_weight2 = jax.random.normal(k_a2, (D_MODEL, D_MODEL), dtype=jnp.float32) * 0.02
        bias = jnp.zeros((D_MODEL,), dtype=jnp.float32)
        return {'x': x, 'weight': weight, 'aux_weight1': aux_weight1, 'aux_weight2': aux_weight2, 'bias': bias}
    _L0_ffn_all = _L0_ffn_setup()
    _L0_ffn_in = {k: v for k, v in _L0_ffn_all.items() if k in ('weight', 'aux_weight1', 'aux_weight2', 'bias')}
    del _L0_ffn_all
    return {'x': x, 'ctx_1024': ctx_1024, 'L0_xattn_in_proj_weight': _L0_xattn_in['in_proj_weight'], 'L0_xattn_in_proj_bias': _L0_xattn_in['in_proj_bias'], 'L0_xattn_out_w': _L0_xattn_in['out_w'], 'L0_xattn_out_b': _L0_xattn_in['out_b'], 'L0_ffn_weight': _L0_ffn_in['weight'], 'L0_ffn_aux_weight1': _L0_ffn_in['aux_weight1'], 'L0_ffn_aux_weight2': _L0_ffn_in['aux_weight2'], 'L0_ffn_bias': _L0_ffn_in['bias']}

def reference(x, ctx_1024, L0_xattn_in_proj_weight, L0_xattn_in_proj_bias, L0_xattn_out_w, L0_xattn_out_b, L0_ffn_weight, L0_ffn_aux_weight1, L0_ffn_aux_weight2, L0_ffn_bias):
    import jax
    import jax.numpy as jnp

    def _L0_xattn_ref(q, k, v, in_proj_weight, in_proj_bias, out_w, out_b):
        import jax, jax.numpy as jnp
        import numpy as np
        EMBED_DIM = 512
        NUM_HEADS = 16
        HEAD_DIM = EMBED_DIM // NUM_HEADS
        B, T, S = (2, 1024, 1024)
        H, D = (NUM_HEADS, HEAD_DIM)
        w_q, w_k, w_v = jnp.split(in_proj_weight, 3, axis=0)
        b_q, b_k, b_v = jnp.split(in_proj_bias, 3, axis=0)
        qp = q @ w_q.T + b_q
        kp = k @ w_k.T + b_k
        vp = v @ w_v.T + b_v
        bsz, t, _ = qp.shape
        s = kp.shape[1]
        qh = qp.reshape(bsz, t, H, D).transpose(0, 2, 1, 3)
        kh = kp.reshape(bsz, s, H, D).transpose(0, 2, 1, 3)
        vh = vp.reshape(bsz, s, H, D).transpose(0, 2, 1, 3)
        scale = D ** (-0.5)
        attn = jnp.einsum('bhtd,bhsd->bhts', qh, kh) * scale
        attn = jax.nn.softmax(attn, axis=-1)
        ctx = jnp.einsum('bhts,bhsd->bhtd', attn, vh)
        ctx = ctx.transpose(0, 2, 1, 3).reshape(bsz, t, H * D)
        out = ctx @ out_w.T + out_b
        return out

    def _L0_ffn_ref(x, weight, aux_weight1, aux_weight2, bias):
        import jax, jax.numpy as jnp
        import numpy as np
        D_MODEL = 512
        h = jnp.einsum('btc,cd->btd', x, weight)
        h = jnp.einsum('btc,cd->btd', h, aux_weight1)
        h = jnp.einsum('btc,cd->btd', h, aux_weight2)
        return jnp.tanh(h + bias)
    x = x + _L0_xattn_ref(_layernorm(x, axis=-1), ctx_1024, ctx_1024, L0_xattn_in_proj_weight, L0_xattn_in_proj_bias, L0_xattn_out_w, L0_xattn_out_b)
    x = x + _L0_ffn_ref(_layernorm(x, axis=-1), L0_ffn_weight, L0_ffn_aux_weight1, L0_ffn_aux_weight2, L0_ffn_bias)
    return x

_drawn_inputs = setup_inputs


def setup_inputs(seed=0):
    import zlib

    import numpy as np

    out = dict(_drawn_inputs(seed))
    spreads = {'L0_xattn_in_proj_bias': (0.0, 0.1),
     'L0_xattn_out_b': (0.0, 0.1),
     'L0_ffn_bias': (0.0, 0.1)}
    factors = {}
    for name, (base, spread) in spreads.items():
        noise = np.random.default_rng([zlib.crc32(name.encode()), seed]).standard_normal(out[name].shape)
        drawn = base * np.exp(spread * noise) if base else spread * noise
        out[name] = jnp.asarray(drawn.astype(out[name].dtype))
    for name, factor in factors.items():
        out[name] = (out[name] * factor).astype(out[name].dtype)
    return out
```

```python
from contextlib import ExitStack

import concourse.bass as bass
from concourse import mybir

F32 = mybir.dt.float32
F32R = mybir.dt.float32r
ACT = mybir.ActivationFunctionType
ALU = mybir.AluOpType
AX = mybir.AxisListType

P = 128
D = 512
C = D // P
H = 16
HD = D // H
HG = P // HD
SUB = 2
TOK = SUB * P
UNROLL = 4
EPS = 1e-5


class Tile:

    def __init__(self, s, i=None):
        self.s, self.i = s, i

    def __add__(self, d):
        return Tile(self.s + d, self.i)

    def __sub__(self, d):
        return Tile(self.s - d, self.i)

    def exists(self, tiles):
        return self.i is not None or 0 <= self.s < tiles


def count(per_tile, tile, k):
    if tile.i is None:
        return per_tile * tile.s + k + 1
    return tile.i * (UNROLL * per_tile) + (per_tile * tile.s + k + 1)


F, XT, Q, O, Z = "ffn", "xn transpose", "query", "out", "z transpose"
BEFORE = [
    [(F, 0, 0), (F, 0, 1)], [(F, 0, 3), (F, 1, 0)], [(F, 1, 2), (F, 1, 3)], [(Q, 0, 1), (O, 0, 0)],
    [(O, 0, 2), (O, 0, 3)], [(O, 1, 1), (O, 1, 2)], [(Q, 1, 0), (Q, 1, 1)], [(Q, 2, 1), (Q, 3, 0)],
]
AFTER = [
    [(F, 0, 2), (XT, 0, 0)], [(F, 1, 1), (XT, 1, 0)], [(Q, 0, 0)], [(O, 0, 1)],
    [(O, 1, 0)], [(O, 1, 3)], [(Q, 2, 0), (Z, 0, 0)], [(Q, 3, 1), (Z, 1, 0)],
]
PARTS = {F: 4, XT: 1, Q: 2, O: 4, Z: 1}
DENSE_BANK = {(F, 0): 5, (XT, 1): 5, (O, 1): 5, (Z, 0): 5,
              (XT, 0): 6, (Q, 0): 6, (Q, 1): 6, (Q, 3): 6,
              (F, 1): 7, (O, 0): 7, (Q, 2): 7, (Z, 1): 7}
BANK_ORDER = {5: [(F, 0), (XT, 1), (O, 1), (Z, 0)],
              6: [(XT, 0), (Q, 0), (Q, 1), (Q, 3)],
              7: [(F, 1), (O, 0), (Q, 2), (Z, 1)]}
SHIFT = {F: -2, XT: 1, Q: 1, O: -1, Z: -1}
CTX_BANK = 4


def build(nc, x, ctx_in, w_in, b_in, w_out, b_out, w_ffn, w_aux1, w_aux2, b_ffn, out):
    B, T, _ = x.shape
    S = ctx_in.shape[1]
    TILES = B * T // TOK
    SCALE = float(HD) ** -0.5
    assert S == P and x.shape[2] == D and UNROLL == B and (TILES - 4) % UNROLL == 0
    LOOPS = (TILES - 4) // UNROLL
    PROLOGUE = [Tile(t) for t in range(-2, 2)]
    EPILOGUE = [Tile(t) for t in range(TILES - 2, TILES + 2)]

    x_view = x.rearrange("b (j s p) d -> b j p s d", s=SUB, p=P)
    out_view = out.rearrange("b (j s p) d -> b j s p d", s=SUB, p=P)

    ctx = ExitStack()
    with ctx:
        def sb(name, shape, dt=F32, where=ctx):
            return where.enter_context(nc.sbuf_tensor(name, shape, dt))

        def sem(name):
            return ctx.enter_context(nc.semaphore(name))

        HI, LO = 0, 1
        wq = [sb(f"wq{h}", [P, C, D], F32R) for h in range(2)]
        wo = [sb(f"wo{h}", [P, C, D], F32R) for h in range(2)]
        wf = [sb(f"wf{h}", [P, C, D], F32R) for h in range(2)]
        keys = sb("keys", [P, B, H // 2, 2, 2 * S], F32R)
        vals = sb("vals", [P, B, D])
        ident = sb("ident", [P, P])
        bo_row = sb("bo_row", [P, D])
        bf_row = sb("bf_row", [P, D])
        bq_col = sb("bq_col", [P, C])
        bk_col = sb("bk_col", [P, C])
        minus_half = sb("minus_half", [P, SUB])
        neg_max = sb("neg_max", [P, 8, HG])
        den = sb("den", [P, 8, HG])
        rden = sb("rden", [P, 8, HG])
        st1 = sb("st1", [P, SUB, 6])
        mv1 = sb("mv1", [P, SUB, 2])
        ve1 = sb("ve1", [P, SUB])
        rstd1 = sb("rstd1", [P, SUB])
        st2 = sb("st2", [P, SUB, 6])
        mv2 = sb("mv2", [P, SUB, 2])
        ve2 = sb("ve2", [P, SUB])
        rstd2 = sb("rstd2", [P, SUB])

        setup = ExitStack()
        with setup:
            ctx_t = sb("ctx_t", [P, C, B * S], where=setup)
            wq_nat = sb("wq_nat", [P, C, D], where=setup)
            wv_nat = sb("wv_nat", [P, C, D], where=setup)
            ctx_nat = sb("ctx_nat", [P, B, D], where=setup)
            wk_nat = sb("wk_nat", [P, C, D], where=setup)
            wk_t = sb("wk_t", [P, C, D], where=setup)
            w0_nat = sb("w0_nat", [P, C, D], where=setup)
            w1_nat = sb("w1_nat", [P, C, D], where=setup)
            w2_nat = sb("w2_nat", [P, C, D], where=setup)
            wo_nat = sb("wo_nat", [P, C, D], where=setup)
            bv_row = sb("bv_row", [P, D], where=setup)
        wv_t, key_hi, key_lo, w0_t, w01_t = wq_nat, ctx_nat, wk_nat, wk_t, w0_nat

        x_sb = sb("x_sb", [P, UNROLL, SUB, D])
        xn = sb("xn", [P, SUB, D])
        work = sb("work", [P, SUB, D])
        xn_t = [sb(f"xn_t{h}", [P, C, TOK], F32R) for h in range(2)]
        q_st = sb("q_st", [P, C, 2, TOK], F32R)
        probs = sb("probs", [P, 2, SUB, HG * S])
        probs_t = sb("probs_t", [P, 2, HG, TOK])
        ctx_o = [sb(f"ctx_o{h}", [P, 2, C, TOK], F32R) for h in range(2)]
        zn_t = [sb(f"zn_t{h}", [P, SUB, C, P], F32R) for h in range(2)]

        ps = ctx.enter_context(nc.psum_tensor("ps", [P, 8, 512], F32))

        consts = sem("consts")
        zeros = sem("zeros")
        loads = [sem(f"load_{n}") for n in ("ctx", "wk", "wq", "wv", "w0", "w1", "w2", "wo", "bias")]
        L_CTX, L_WK, L_WQ, L_WV, L_W0, L_W1, L_W2, L_WO, L_B = loads
        s_mm = sem("s_mm")
        s_act = sem("s_act")
        s_dve = sem("s_dve")
        s_key = sem("s_key")
        s_blocks = sem("s_blocks")
        x_in = [sem(f"x_in{j}") for j in range(UNROLL)]
        stored = [sem(f"stored{s}") for s in range(SUB)]
        scores_ready = sem("scores_ready")
        pt_ready = sem("pt_ready")
        ctx_ready = sem("ctx_ready")
        dense_ready = {F: sem("f_ready"), XT: sem("xt_ready"), Q: sem("q_ready"),
                       O: sem("o_ready"), Z: sem("z_ready")}
        exp_done = sem("exp_done")
        pt_act = sem("pt_act")
        pt_dve = sem("pt_dve")
        xn_hi = sem("xn_hi")
        q_hi = sem("q_hi")
        ctx_hi = sem("ctx_hi")
        zn_hi = sem("zn_hi")
        tanh_done = sem("tanh_done")
        max_done = sem("max_done")
        rden_done = sem("rden_done")
        xn_lo = sem("xn_lo")
        q_lo = sem("q_lo")
        ctx_lo = sem("ctx_lo")
        zn_lo = sem("zn_lo")
        arg_done = sem("arg_done")
        y_done = sem("y_done")
        mv1_done = sem("mv1_done")
        ve1_done = sem("ve1_done")
        mv2_done = sem("mv2_done")
        ve2_done = sem("ve2_done")
        xn_done = sem("xn_done")
        zn_done = sem("zn_done")
        rstd1_done = sem("rstd1_done")
        rstd2_done = sem("rstd2_done")
        xb_done = sem("xb_done")
        probs_ready = sem("probs_ready")
        out_done = sem("out_done")

        freed_by = {F: (arg_done, 2), XT: (xn_lo, 2), Q: (q_lo, 4), O: (y_done, 2), Z: (zn_lo, 2)}

        def wait(eng, semaphore, per_tile, tile, k):
            if tile.exists(TILES):
                eng.wait_ge(semaphore, count(per_tile, tile, k))

        def last_user(t, kind, n):
            order = BANK_ORDER[DENSE_BANK[kind, n]]
            k = order.index((kind, n))
            for back in range(1, 3 * len(order)):
                kind_b, n_b = order[(k - back) % len(order)]
                tile = t + (k - back) // len(order) + SHIFT[kind_b]
                if tile.exists(TILES):
                    return kind_b, n_b, tile
            return None

        plan = ([("ctx_t", c, "ad"[c % 2]) for c in range(C)] + [("wk_t", c, "ad"[c % 2]) for c in range(C)]
                + [("wq_t", c, "ad") for c in range(C)] + [("key", c, "k") for c in range(C)]
                + [("wv_t", c, "ad"[c % 2]) for c in range(C)] + [("val", b, "d") for b in range(B)]
                + [("w0_t", c, "ad"[c % 2]) for c in range(C)] + [("w01_t", c, "ad"[c % 2]) for c in range(C)]
                + [("wf", c, "ad") for c in range(C)] + [("wo_t", c, "ad") for c in range(C)])
        names = [(name, c) for name, c, _ in plan]
        on_act = [how in ("a", "ad", "k") for _, _, how in plan]
        on_dve = [how in ("d", "ad", "k") for _, _, how in plan]

        def setup_copied(eng, m):
            if on_act[m]:
                eng.wait_ge(s_act, sum(on_act[:m + 1]))
            if on_dve[m]:
                eng.wait_ge(s_dve, sum(on_dve[:m + 1]))

        def setup_all(eng, name):
            for m, (n, _) in enumerate(names):
                if n == name and (m + 1 == len(names) or names[m + 1][0] != name or m and names[m - 1][0] == name):
                    setup_copied(eng, m)

        def setup_done(eng):
            eng.wait_ge(s_act, sum(on_act))
            eng.wait_ge(s_dve, sum(on_dve))
            eng.wait_ge(s_blocks, 16 * C * HG * 4)

        block = ctx.enter_context(nc.Block())

        @block.sync
        def _(sp):
            def chunked(w):
                return w.rearrange("(c p) d -> p c d", p=P)

            sp.dma_start(ctx_nat[:], ctx_in.rearrange("b s d -> s b d")).then_inc(L_CTX, 16)
            sp.dma_start(wk_nat[:], chunked(w_in[D:2 * D, :])).then_inc(L_WK, 16)
            sp.dma_start(wq_nat[:], chunked(w_in[0:D, :])).then_inc(L_WQ, 16)
            sp.dma_start(wv_nat[:], chunked(w_in[2 * D:3 * D, :])).then_inc(L_WV, 16)
            sp.dma_start(w0_nat[:], chunked(w_ffn)).then_inc(L_W0, 16)
            sp.dma_start(w1_nat[:], chunked(w_aux1)).then_inc(L_W1, 16)
            sp.dma_start(w2_nat[:], chunked(w_aux2)).then_inc(L_W2, 16)
            sp.dma_start(wo_nat[:], chunked(w_out)).then_inc(L_WO, 16)

            sp.wait_ge(zeros, 2)
            for c in range(C):
                setup_copied(sp, names.index(("key", c)))
                for j in range(HG):
                    pair, h = 2 * c + j // 2, j % 2
                    for half, kc in ((HI, key_hi), (LO, key_lo)):
                        for row in (HD * h, P // 2 + HD * h):
                            sp.dma_start(
                                keys[row:row + HD, :, pair, half, h * S:(h + 1) * S].bitcast(F32),
                                kc[HD * j:HD * (j + 1), c, :].rearrange("p (b s) -> p b s", b=B),
                            ).then_inc(s_blocks, 16)

            def load(t):
                j = t.s // UNROLL if t.i is None else t.i + t.s // UNROLL
                sp.dma_start(x_sb[:, t.s % UNROLL], x_view[t.s % B, j]).then_inc(x_in[t.s % UNROLL], 16)

            setup_done(sp)
            for t in range(UNROLL):
                load(Tile(t))

            def iteration(t):
                done, more = t - 2, t + 2
                for s in range(SUB):
                    if done.exists(TILES):
                        wait(sp, out_done, 2, done, s)
                        j = done.s // UNROLL if t.i is None else t.i + done.s // UNROLL
                        sp.dma_start(out_view[done.s % B, j, s], work[:, s]).then_inc(stored[s], 16)
                if done.exists(TILES) and more.exists(TILES):
                    load(more)

            for t in PROLOGUE:
                iteration(t)
            with sp.Fori(0, LOOPS) as i:
                for k in range(UNROLL):
                    iteration(Tile(2 + k, i))
            for t in EPILOGUE:
                iteration(t)
            for s in range(SUB):
                sp.wait_ge(stored[s], 16 * TILES)

        @block.gpsimd
        def _(pool):
            nc.gpsimd.memset(ident[:], 0.0).then_inc(consts, 1)
            nc.gpsimd.memset(minus_half[:], -0.5).then_inc(consts, 1)
            pool.wait_ge(consts, 2)
            nc.gpsimd.affine_select(out=ident[:], in_=ident[:], compare_op=ALU.not_equal, fill=1.0, base=0,
                                    pattern=[[-1, P]], channel_multiplier=1).then_inc(consts, 1)
            for h in range(2):
                nc.gpsimd.memset(keys[:, h * B // 2:(h + 1) * B // 2].bitcast(F32), 0.0).then_inc(zeros, 1)
            pool.wait_ge(L_B, 16 * 5)
            setup_done(pool)

            def normalise_probs(t, n):
                g, s = n // 2, n % 2
                wait(pool, rden_done, 8, t, n)
                pr = probs[:, g % 2, s].rearrange("p (h k) -> p h k", h=HG)
                nc.gpsimd.tensor_tensor(pr, pr, rden[:, n].unsqueeze(2).to_broadcast([P, HG, S]),
                                        ALU.mult).then_inc(probs_ready, 1)

            def iteration(t):
                add, done, prev, more = t + 1, t - 2, t - 1, t + 2
                for n in range(8):
                    if n < SUB and add.exists(TILES):
                        wait(pool, xn_done, 2, add, n)
                        xs = x_sb[:, add.s % UNROLL, n]
                        nc.gpsimd.tensor_tensor(xs, xs, bo_row[:], ALU.add).then_inc(xb_done, 1)
                    if n in (2, 3) and done.exists(TILES):
                        s = n - 2
                        wait(pool, tanh_done, 2, done, s)
                        nc.gpsimd.tensor_tensor(work[:, s], work[:, s], x_sb[:, done.s % UNROLL, s],
                                                ALU.add).then_inc(out_done, 1)
                    if n in (5, 6) and prev.exists(TILES):
                        s = n - 5
                        wait(pool, ve2_done, 2, prev, s)
                        nc.gpsimd.tensor_tensor(rstd2[:, s:s + 1], ve2[:, s:s + 1], minus_half[:, 0:1],
                                                ALU.pow).then_inc(rstd2_done, 1)
                    if n == 5 and more.exists(TILES):
                        wait(pool, ve1_done, 1, more, 0)
                        nc.gpsimd.tensor_tensor(rstd1[:], ve1[:], minus_half[:], ALU.pow).then_inc(rstd1_done, 1)
                    if t.exists(TILES):
                        normalise_probs(t, n)

            for t in PROLOGUE:
                iteration(t)
            with pool.Fori(0, LOOPS) as i:
                for k in range(UNROLL):
                    iteration(Tile(2 + k, i))
            for t in EPILOGUE:
                iteration(t)

        @block.scalar
        def _(act):
            def column(v):
                return v.rearrange("(c p) -> p c", p=P)

            act.dma_start(bq_col[:], column(b_in[0:D]), allow_slow_non_contiguous=True).then_inc(L_B, 16)
            act.dma_start(bk_col[:], column(b_in[D:2 * D]), allow_slow_non_contiguous=True).then_inc(L_B, 16)
            act.dma_start(bv_row[:], b_in[2 * D:3 * D].partition_broadcast(P)).then_inc(L_B, 16)
            act.dma_start(bo_row[:], b_out.partition_broadcast(P)).then_inc(L_B, 16)
            act.dma_start(bf_row[:], b_ffn.partition_broadcast(P)).then_inc(L_B, 16)

            hi_of = {"wq_t": wq[HI], "wf": wf[HI], "wo_t": wo[HI], "ctx_t": ctx_t, "wk_t": wk_t,
                     "wv_t": wv_t, "w0_t": w0_t, "w01_t": w01_t}
            keys_seen = 0
            for m, (name, c, how) in enumerate(plan):
                if not on_act[m]:
                    continue
                act.wait_ge(s_mm, m + 1)
                if name == "key":
                    keys_seen += 1
                    act.wait_ge(s_key, keys_seen)
                    dst = key_hi[:, c].bitcast(F32R)
                else:
                    dst = hi_of[name][:, c]
                nc.scalar.copy(dst, ps[:, m % 8]).then_inc(s_act, 1)
            act.wait_ge(L_B, 16 * 5)
            setup_done(act)

            def exps(t, n):
                g, s = n // 2, n % 2
                wait(act, max_done, 8, t, n)
                wait(act, pt_ready, 8, t if g >= 2 else t - 1, 2 * g - 3 if g >= 2 else 2 * g + 5)
                for h in range(HG):
                    last = nc.scalar.activation(probs[:, g % 2, s, h * S:(h + 1) * S],
                                                ps[:, n % 2, h * S:(h + 1) * S], ACT.Exp,
                                                bias=neg_max[:, n, h:h + 1], accum_out=den[:, n, h:h + 1])
                last.then_inc(exp_done, 1)

            def copy_probs_t(t, idx):
                g = idx // 2
                if t.exists(TILES):
                    wait(act, pt_ready, 8, t, idx)
                    wait(act, ctx_ready, 4, t if g >= 2 else t - 1, (g - 2) % 4)
                    nc.scalar.copy(probs_t[:, g % 2, 2:4].rearrange("p h t -> p (h t)"),
                                   ps[:, 2 + idx % 2]).then_inc(pt_act, 1)

            def context_hi(t, g):
                if t.exists(TILES):
                    wait(act, ctx_ready, 4, t, g)
                    wait(act, dense_ready[O], 2, t - 2, 1)
                    nc.scalar.copy(ctx_o[HI][:, t.s % 2, g], ps[:, CTX_BANK, 0:TOK]).then_inc(ctx_hi, 1)

            def xn_t_hi(t, s):
                if t.exists(TILES):
                    wait(act, dense_ready[XT], 2, t, s)
                    wait(act, dense_ready[Q], 4, t - 1, C - 1)
                    nc.scalar.copy(xn_t[HI][:, :, s * P:(s + 1) * P],
                                   ps[:, DENSE_BANK[XT, s]].rearrange("p (c t) -> p c t", c=C)).then_inc(xn_hi, 1)

            def query_hi(t, c):
                if t.exists(TILES):
                    wait(act, dense_ready[Q], 4, t, c)
                    wait(act, scores_ready, 8, t - 1, 2 * c + 1)
                    for pair in range(2):
                        rows = slice(pair * P // 2, (pair + 1) * P // 2)
                        last = nc.scalar.activation(q_st[rows, c, pair], ps[rows, DENSE_BANK[Q, c], 0:TOK],
                                                    ACT.Identity, bias=bq_col[rows, c:c + 1])
                    last.then_inc(q_hi, 1)

            def z_t_hi(t, s):
                if t.exists(TILES):
                    wait(act, dense_ready[Z], 2, t, s)
                    wait(act, dense_ready[F], 2, t - 1, s)
                    nc.scalar.copy(zn_t[HI][:, s].rearrange("p c t -> p (c t)"),
                                   ps[:, DENSE_BANK[Z, s]]).then_inc(zn_hi, 1)

            def tanh(t, s):
                if t.exists(TILES):
                    wait(act, arg_done, 2, t, s)
                    nc.scalar.activation(work[:, s], work[:, s], ACT.Tanh).then_inc(tanh_done, 1)

            def iteration(t):
                for n in range(8):
                    if n == 0:
                        query_hi(t, 3)
                        z_t_hi(t - 2, 1)
                    if n == 1:
                        xn_t_hi(t + 1, 0)
                    if n == 2:
                        xn_t_hi(t + 1, 1)
                    if n == 3:
                        tanh(t - 2, 1)
                    if n == 7:
                        z_t_hi(t - 1, 0)
                    if t.exists(TILES):
                        exps(t, n)
                    if n == 0:
                        context_hi(t - 1, 2)
                    if n == 1:
                        copy_probs_t(t - 1, 7)
                        tanh(t - 2, 0)
                    if n == 2:
                        context_hi(t - 1, 3)
                    if n == 3:
                        query_hi(t + 1, 0)
                    if n in (4, 6):
                        context_hi(t, n // 2 - 2)
                    if n == 6:
                        query_hi(t + 1, 1)
                    if n == 7:
                        query_hi(t + 1, 2)
                    if n in (3, 5, 7):
                        copy_probs_t(t, n - 2)

            for t in PROLOGUE:
                iteration(t)
            with act.Fori(0, LOOPS) as i:
                for k in range(UNROLL):
                    iteration(Tile(2 + k, i))
            for t in EPILOGUE:
                iteration(t)

        @block.vector
        def _(dve):
            dve.wait_ge(L_B, 16 * 5)
            lo_of = {"wq_t": wq, "wf": wf, "wo_t": wo}
            copy_of = {"ctx_t": ctx_t, "wk_t": wk_t, "wv_t": wv_t, "w0_t": w0_t, "w01_t": w01_t}
            keys_seen = 0
            for m, (name, c, how) in enumerate(plan):
                if not on_dve[m]:
                    continue
                dve.wait_ge(s_mm, m + 1)
                bank = ps[:, m % 8]
                if name == "key":
                    nc.vector.tensor_scalar(bank, bank, bk_col[:, c:c + 1], SCALE, ALU.add, ALU.mult).then_inc(s_key, 1)
                    keys_seen += 1
                    dve.wait_ge(s_key, keys_seen)
                if how in ("ad", "k"):
                    dve.wait_ge(s_act, sum(on_act[:m + 1]))
                    hi, lo = ((key_hi[:, c], key_lo[:, c].bitcast(F32R)) if name == "key" else
                              (lo_of[name][HI][:, c].bitcast(F32), lo_of[name][LO][:, c]))
                    nc.vector.tensor_tensor(lo, bank, hi, ALU.subtract).then_inc(s_dve, 1)
                elif name == "val":
                    nc.vector.tensor_tensor(vals[:, c], bank, bv_row[:], ALU.add).then_inc(s_dve, 1)
                else:
                    nc.vector.tensor_copy(copy_of[name][:, c], bank).then_inc(s_dve, 1)
            setup_done(dve)

            def maxima(t, n):
                wait(dve, scores_ready, 8, t, n)
                nc.vector.tensor_reduce(neg_max[:, n], ps[:, n % 2].rearrange("p (h k) -> p h k", h=HG),
                                        AX.X, ALU.max, negate=True).then_inc(max_done, 1)

            def reciprocals(t, n):
                wait(dve, exp_done, 8, t, n)
                nc.vector.reciprocal(rden[:, n], den[:, n]).then_inc(rden_done, 1)

            def copy_probs_t(t, idx):
                g = idx // 2
                if t.exists(TILES):
                    wait(dve, pt_ready, 8, t, idx)
                    wait(dve, ctx_ready, 4, t if g >= 2 else t - 1, (g - 2) % 4)
                    nc.vector.tensor_copy(probs_t[:, g % 2, 0:2].rearrange("p h t -> p (h t)"),
                                          ps[:, 2 + idx % 2]).then_inc(pt_dve, 1)

            def context_lo(t, g):
                if t.exists(TILES):
                    wait(dve, ctx_hi, 4, t, g)
                    nc.vector.tensor_tensor(ctx_o[LO][:, t.s % 2, g], ps[:, CTX_BANK, 0:TOK],
                                            ctx_o[HI][:, t.s % 2, g].bitcast(F32), ALU.subtract).then_inc(ctx_lo, 1)

            def xn_t_lo(t, s):
                if t.exists(TILES):
                    wait(dve, xn_hi, 2, t, s)
                    cols = slice(s * P, (s + 1) * P)
                    nc.vector.tensor_tensor(xn_t[LO][:, :, cols],
                                            ps[:, DENSE_BANK[XT, s]].rearrange("p (c t) -> p c t", c=C),
                                            xn_t[HI][:, :, cols].bitcast(F32), ALU.subtract).then_inc(xn_lo, 1)

            def query_lo(t, c):
                if t.exists(TILES):
                    wait(dve, q_hi, 4, t, c)
                    for pair in range(2):
                        rows = slice(pair * P // 2, (pair + 1) * P // 2)
                        other = slice((1 - pair) * P // 2, (2 - pair) * P // 2)
                        last = nc.vector.scalar_tensor_tensor(
                            out=q_st[other, c, pair], in0=ps[rows, DENSE_BANK[Q, c], 0:TOK],
                            scalar=bq_col[rows, c:c + 1], in1=q_st[rows, c, pair].bitcast(F32),
                            op0=ALU.add, op1=ALU.subtract)
                    last.then_inc(q_lo, 1)

            def z_t_lo(t, s):
                if t.exists(TILES):
                    wait(dve, zn_hi, 2, t, s)
                    nc.vector.tensor_tensor(zn_t[LO][:, s].rearrange("p c t -> p (c t)"), ps[:, DENSE_BANK[Z, s]],
                                            zn_t[HI][:, s].rearrange("p c t -> p (c t)").bitcast(F32),
                                            ALU.subtract).then_inc(zn_lo, 1)

            def tanh_argument(t, s):
                if t.exists(TILES):
                    wait(dve, dense_ready[F], 2, t, s)
                    nc.vector.tensor_tensor(work[:, s], ps[:, DENSE_BANK[F, s]], bf_row[:], ALU.add).then_inc(arg_done, 1)

            def x_statistics(t):
                if t.exists(TILES):
                    slot = t.s % UNROLL
                    turns = t.s // UNROLL + 1 if t.i is None else t.i + (t.s // UNROLL + 1)
                    dve.wait_ge(x_in[slot], turns * 16)
                    wait(dve, rstd1_done, 1, t - 1, 0)
                    for s in range(SUB):
                        nc.vector.bn_stats(st1[:, s], x_sb[:, slot, s])
                    nc.vector.drain()
                    for s in range(SUB):
                        nc.vector.bn_aggr(mv1[:, s], st1[:, s]).then_inc(mv1_done, 1)
                    wait(dve, mv1_done, 2, t, 1)
                    nc.vector.tensor_scalar_add(ve1[:], mv1[:, :, 1], EPS).then_inc(ve1_done, 1)

            def x_normalise(t):
                if t.exists(TILES):
                    wait(dve, rstd1_done, 1, t, 0)
                    for s in range(SUB):
                        wait(dve, dense_ready[XT], 2, t - 1, s)
                        nc.vector.tensor_scalar(xn[:, s], x_sb[:, t.s % UNROLL, s], mv1[:, s, 0:1],
                                                rstd1[:, s:s + 1], ALU.subtract, ALU.mult).then_inc(xn_done, 1)

            def residual(t, s):
                if t.exists(TILES):
                    xs = x_sb[:, t.s % UNROLL, s]
                    wait(dve, dense_ready[O], 2, t, s)
                    wait(dve, xb_done, 2, t, s)
                    nc.vector.tensor_tensor(xs, ps[:, DENSE_BANK[O, s]], xs, ALU.add).then_inc(y_done, 1)
                    wait(dve, y_done, 2, t, s)
                    nc.vector.bn_stats(st2[:, s], xs)

            def y_statistics(t, s):
                if t.exists(TILES):
                    nc.vector.drain()
                    nc.vector.bn_aggr(mv2[:, s], st2[:, s]).then_inc(mv2_done, 1)
                    wait(dve, mv2_done, 2, t, s)
                    nc.vector.tensor_scalar_add(ve2[:, s:s + 1], mv2[:, s, 1:2], EPS).then_inc(ve2_done, 1)

            def y_normalise(t, s):
                if t.exists(TILES):
                    wait(dve, rstd2_done, 2, t, s)
                    if (t - 1).exists(TILES):
                        dve.wait_ge(stored[s], 16 * t.s if t.i is None else t.i * (16 * UNROLL) + 16 * t.s)
                    nc.vector.tensor_scalar(work[:, s], x_sb[:, t.s % UNROLL, s], mv2[:, s, 0:1],
                                            rstd2[:, s:s + 1], ALU.subtract, ALU.mult).then_inc(zn_done, 1)

            def iteration(t):
                for n in range(8):
                    if t.exists(TILES):
                        maxima(t, n)
                    if n == 0:
                        query_lo(t, 3)
                        z_t_lo(t - 2, 1)
                    if n == 1:
                        xn_t_lo(t + 1, 0)
                        tanh_argument(t - 2, 0)
                    if n == 2:
                        xn_t_lo(t + 1, 1)
                        tanh_argument(t - 2, 1)
                    if n == 4:
                        residual(t - 1, 0)
                    if n == 5:
                        x_statistics(t + 2)
                    if n == 6:
                        residual(t - 1, 1)
                    if n == 7:
                        y_normalise(t - 1, 1)
                        z_t_lo(t - 1, 0)
                    if t.exists(TILES):
                        reciprocals(t, n)
                    if n == 0:
                        context_lo(t - 1, 2)
                        copy_probs_t(t - 1, 6)
                    if n == 2:
                        context_lo(t - 1, 3)
                        copy_probs_t(t, 0)
                    if n == 3:
                        query_lo(t + 1, 0)
                    if n == 4:
                        y_statistics(t - 1, 0)
                        context_lo(t, 0)
                        copy_probs_t(t, 2)
                    if n == 5:
                        y_normalise(t - 1, 0)
                    if n == 6:
                        y_statistics(t - 1, 1)
                        context_lo(t, 1)
                        copy_probs_t(t, 4)
                        query_lo(t + 1, 1)
                    if n == 7:
                        query_lo(t + 1, 2)
                        x_normalise(t + 2)

            for t in PROLOGUE:
                iteration(t)
            with dve.Fori(0, LOOPS) as i:
                for k in range(UNROLL):
                    iteration(Tile(2 + k, i))
            for t in EPILOGUE:
                iteration(t)

        @block.tensor
        def _(pe):
            pe.wait_ge(consts, 3)
            nat = {"ctx_t": (ctx_nat, L_CTX), "wk_t": (wk_nat, L_WK), "wq_t": (wq_nat, L_WQ),
                   "wv_t": (wv_nat, L_WV), "w0_t": (w0_nat, L_W0), "wo_t": (wo_nat, L_WO)}

            def product(bank, lhs_t, rhs):
                for c in range(C):
                    last = nc.tensor.matmul(bank, lhs_t[c], rhs[c], start=(c == 0), stop=(c == C - 1))
                return last

            for m, (name, c, how) in enumerate(plan):
                bank = ps[:, m % 8]
                if m >= 8:
                    setup_copied(pe, m - 8)
                cols = slice(c * P, (c + 1) * P)
                if name in nat:
                    src, loaded = nat[name]
                    if c == 0:
                        pe.wait_ge(loaded, 16)
                    if name == "wv_t" and c == 0:
                        setup_all(pe, "wq_t")
                    for r in range(C):
                        last = nc.tensor.transpose(bank[:, r * P:(r + 1) * P], src[:, r, cols], ident[:])
                elif name == "key":
                    if c == 0:
                        setup_all(pe, "ctx_t")
                        setup_all(pe, "wk_t")
                    last = product(bank, [wk_t[:, k, cols] for k in range(C)], [ctx_t[:, k] for k in range(C)])
                elif name == "val":
                    if c == 0:
                        setup_all(pe, "wv_t")
                    last = product(bank, [ctx_t[:, k, cols] for k in range(C)], [wv_t[:, k] for k in range(C)])
                elif name == "w01_t":
                    if c == 0:
                        pe.wait_ge(L_W1, 16)
                        setup_all(pe, "w0_t")
                    last = product(bank, [w1_nat[:, k, cols] for k in range(C)], [w0_t[:, k] for k in range(C)])
                elif name == "wf":
                    if c == 0:
                        pe.wait_ge(L_W2, 16)
                        setup_all(pe, "w01_t")
                    last = product(bank, [w01_t[:, k, cols] for k in range(C)], [w2_nat[:, k] for k in range(C)])
                last.then_inc(s_mm, 1)
            setup_done(pe)

            PASSES = [(half, k) for half in ((HI, HI), (LO, HI), (HI, LO)) for k in range(C)]

            def scores(t, n):
                g, s = n // 2, n % 2
                wait(pe, q_lo, 4, t, g)
                wait(pe, exp_done, 8, t if n >= 2 else t - 1, (n - 2) % 8)
                for pair in range(2):
                    for half in (HI, LO):
                        last = nc.tensor.matmul(ps[:, n % 2, pair * 2 * S:(pair + 1) * 2 * S],
                                                q_st[:, g, pair, s * P:(s + 1) * P],
                                                keys[:, t.s % B, 2 * g + pair, half],
                                                start=(half == HI), stop=(half == LO))
                last.then_inc(scores_ready, 1)

            def transpose_probs(t, idx):
                if not t.exists(TILES):
                    return
                g, pair = idx // 2, idx % 2
                wait(pe, probs_ready, 8, t, 2 * g + 1)
                wait(pe, pt_dve if idx % 2 == 0 else pt_act, 4, t if g else t - 1, (g - 1) % 4)
                for h in range(2):
                    for s in range(SUB):
                        col = (2 * pair + h) * S
                        last = nc.tensor.transpose(ps[:, 2 + idx % 2, (h * SUB + s) * P:(h * SUB + s + 1) * P],
                                                   probs[:, g % 2, s, col:col + S], ident[:])
                last.then_inc(pt_ready, 1)

            def context(t, g):
                if not t.exists(TILES):
                    return
                wait(pe, pt_dve, 4, t, g)
                wait(pe, pt_act, 4, t, g)
                wait(pe, ctx_lo, 4, t if g else t - 1, (g - 1) % 4)
                for h in range(HG):
                    f = (g * HG + h) * HD
                    last = nc.tensor.matmul(ps[HD * h:HD * (h + 1), CTX_BANK, 0:TOK],
                                            vals[:, t.s % B, f:f + HD], probs_t[:, g % 2, h],
                                            start=True, stop=True, tile_position=(0, HD * h))
                last.then_inc(ctx_ready, 1)

            def dense(t_iter, kind, n, part):
                t = t_iter + SHIFT[kind]
                if not t.exists(TILES):
                    return
                bank = ps[:, DENSE_BANK[kind, n]]
                if part == 0:
                    before = last_user(t_iter, kind, n)
                    if before:
                        freed, per_tile = freed_by[before[0]]
                        wait(pe, freed, per_tile, before[2], before[1])
                if kind in (XT, Z):
                    src, ready = (xn, xn_done) if kind == XT else (work, zn_done)
                    wait(pe, ready, 2, t, n)
                    for c in range(C):
                        last = nc.tensor.transpose(bank[:, c * P:(c + 1) * P], src[:, n, c * P:(c + 1) * P], ident[:])
                    last.then_inc(dense_ready[kind], 1)
                    return
                if kind == Q:
                    if part == 0:
                        wait(pe, xn_lo, 2, t, 1)
                    dst = bank[:, 0:TOK]
                elif kind == O:
                    if part == 0:
                        wait(pe, ctx_lo, 4, t, C - 1)
                    dst = bank
                else:
                    if part == 0:
                        wait(pe, zn_lo, 2, t, n)
                    dst = bank
                size = len(PASSES) // PARTS[kind]
                for j in range(part * size, (part + 1) * size):
                    (a, w), k = PASSES[j]
                    if kind == Q:
                        lhs, rhs = wq[w][:, k, n * P:(n + 1) * P], xn_t[a][:, k]
                    elif kind == O:
                        lhs, rhs = ctx_o[a][:, t.s % 2, k, n * P:(n + 1) * P], wo[w][:, k]
                    else:
                        lhs, rhs = zn_t[a][:, n, k], wf[w][:, k]
                    last = nc.tensor.matmul(dst, lhs, rhs, start=(j == 0), stop=(j == len(PASSES) - 1))
                if part == PARTS[kind] - 1:
                    last.then_inc(dense_ready[kind], 1)

            def iteration(t):
                for n in range(8):
                    if t.exists(TILES):
                        scores(t, n)
                    for item in BEFORE[n]:
                        dense(t, *item)
                    if n % 2 == 0:
                        context(t - 1 if n < 4 else t, (n // 2 + 2) % 4)
                    transpose_probs(t - 1 if n < 2 else t, (n - 2) % 8)
                    for item in AFTER[n]:
                        dense(t, *item)

            for t in PROLOGUE:
                iteration(t)
            with pe.Fori(0, LOOPS) as i:
                for k in range(UNROLL):
                    iteration(Tile(2 + k, i))
            for t in EPILOGUE:
                iteration(t)


_INS = ["x", "ctx_1024", "L0_xattn_in_proj_weight", "L0_xattn_in_proj_bias", "L0_xattn_out_w", "L0_xattn_out_b",
        "L0_ffn_weight", "L0_ffn_aux_weight1", "L0_ffn_aux_weight2", "L0_ffn_bias"]


def kernel(**inputs):
    import numpy as _np
    import concourse.bacc as _bacc
    from concourse import mybir as _mybir
    from concourse.bass_utils import run_bass_kernel_spmd as _run

    nc = _bacc.Bacc("TRN2", target_bir_lowering=False, num_devices=1)
    arrays, args = {}, []
    for name in _INS:
        a = _np.ascontiguousarray(inputs[name])
        arrays[f"in_{name}"] = a
        args.append(nc.dram_tensor(f"in_{name}", a.shape, _mybir.dt.from_np(a.dtype), kind="ExternalInput").ap())
    shape = inputs["x"].shape
    args.append(nc.dram_tensor("out_y", shape, _mybir.dt.float32, kind="ExternalOutput").ap())
    build(nc, *args)
    r = _run(nc, [arrays], core_ids=[0])
    return r.results[0]["out_y"]
```

```python
from contextlib import ExitStack

import concourse.bass as bass
from concourse import mybir

F32 = mybir.dt.float32
F32R = mybir.dt.float32r
ACT = mybir.ActivationFunctionType
ALU = mybir.AluOpType
AX = mybir.AxisListType

P = 128
D = 512
C = D // P
H = 16
HD = D // H
HG = P // HD
SUB = 2
TOK = SUB * P
UNROLL = 4
EPS = 1e-5


class Tile:

    def __init__(self, s, i=None):
        self.s, self.i = s, i

    def __add__(self, d):
        return Tile(self.s + d, self.i)

    def __sub__(self, d):
        return Tile(self.s - d, self.i)

    def exists(self, tiles):
        return self.i is not None or 0 <= self.s < tiles


def count(per_tile, tile, k):
    if tile.i is None:
        return per_tile * tile.s + k + 1
    return tile.i * (UNROLL * per_tile) + (per_tile * tile.s + k + 1)


F, XT, Q, O, Z0, Z1 = "ffn", "xn transpose", "query", "out", "z transpose 0", "z transpose 1"
PARTS = {F: 4, XT: 1, Q: 2, O: 4, Z0: 1, Z1: 1}
SHIFT = {F: -2, XT: 1, Q: 1, O: -1, Z0: -1, Z1: -2}
CTX_BANK = 4
BANK = {('ffn', 0): 5,
 ('ffn', 1): 6,
 ('out', 0): 7,
 ('out', 1): 7,
 ('query', 0): 5,
 ('query', 1): 6,
 ('query', 2): 6,
 ('query', 3): 7,
 ('xn transpose', 0): 7,
 ('xn transpose', 1): 5,
 ('z transpose 0', 0): 5,
 ('z transpose 1', 0): 6}
ORD = {'act': [('q', 0, 3), ('ctx', -1, 2), ('exp', 0, 0), ('z', -2, 1), ('xt', 1, 0), ('exp', 0, 1), ('pt', -1, 7),
         ('xt', 1, 1), ('tanh', -2, 0), ('exp', 0, 2), ('ctx', -1, 3), ('tanh', -2, 1), ('exp', 0, 3),
         ('pt', 0, 1), ('q', 1, 0), ('exp', 0, 4), ('ctx', 0, 0), ('q', 1, 1), ('pt', 0, 3), ('exp', 0, 5),
         ('ctx', 0, 1), ('exp', 0, 6), ('z', -1, 0), ('exp', 0, 7), ('q', 1, 2), ('pt', 0, 5)],
 'dve': [('max', 0, 0), ('q', 0, 3), ('z', -2, 1), ('max', 0, 1), ('rec', 0, 0), ('arg', -2, 0), ('pt', -1, 6),
         ('ctx', -1, 2), ('max', 0, 2), ('rec', 0, 1), ('xt', 1, 0), ('xt', 1, 1), ('arg', -2, 1),
         ('rec', 0, 2), ('ctx', -1, 3), ('pt', 0, 0), ('max', 0, 3), ('rec', 0, 3), ('max', 0, 4), ('q', 1, 0),
         ('y', -1, 0), ('ctx', 0, 0), ('pt', 0, 2), ('max', 0, 5), ('rec', 0, 4), ('ys', -1, 0), ('xs', 2, 0),
         ('rec', 0, 5), ('q', 1, 1), ('max', 0, 6), ('yn', -1, 0), ('xn', 2, 0), ('y', -1, 1), ('max', 0, 7),
         ('rec', 0, 6), ('ys', -1, 1), ('ctx', 0, 1), ('pt', 0, 4), ('z', -1, 0), ('yn', -1, 1), ('xn', 2, 1),
         ('rec', 0, 7), ('q', 1, 2)],
 'pe': [('S', 0, 0), ('ffn', 0, 0), ('ffn', 0, 1), ('C', -1, 2), ('z transpose 1', 0, 0), ('T', -1, 6),
        ('ffn', 0, 2), ('xn transpose', 0, 0), ('S', 0, 1), ('T', -1, 7), ('ffn', 0, 3), ('ffn', 1, 0),
        ('S', 0, 2), ('xn transpose', 1, 0), ('ffn', 1, 1), ('ffn', 1, 2), ('ffn', 1, 3), ('C', -1, 3),
        ('T', 0, 0), ('query', 0, 0), ('S', 0, 3), ('query', 0, 1), ('out', 0, 0), ('S', 0, 4), ('T', 0, 1),
        ('out', 0, 1), ('out', 0, 2), ('out', 0, 3), ('C', 0, 0), ('T', 0, 2), ('query', 1, 0), ('S', 0, 5),
        ('query', 1, 1), ('T', 0, 3), ('out', 1, 0), ('out', 1, 1), ('out', 1, 2), ('C', 0, 1), ('S', 0, 6),
        ('out', 1, 3), ('T', 0, 4), ('z transpose 0', 0, 0), ('S', 0, 7), ('query', 2, 0), ('T', 0, 5),
        ('query', 2, 1), ('query', 3, 0), ('query', 3, 1)],
 'pool': [('bias', 1, 0), ('norm', 0, 0), ('norm', 0, 1), ('res', -2, 0), ('norm', 0, 2), ('bias', 1, 1),
          ('res', -2, 1), ('norm', 0, 3), ('norm', 0, 4), ('yr', -1, 0), ('norm', 0, 5), ('xr', 2, 0),
          ('norm', 0, 6), ('yr', -1, 1), ('norm', 0, 7)]}


def build(nc, x, ctx_in, w_in, b_in, w_out, b_out, w_ffn, w_aux1, w_aux2, b_ffn, out):
    B, T, _ = x.shape
    S = ctx_in.shape[1]
    TILES = B * T // TOK
    SCALE = float(HD) ** -0.5
    assert S == P and x.shape[2] == D and UNROLL == B and (TILES - 4) % UNROLL == 0
    LOOPS = (TILES - 4) // UNROLL
    PROLOGUE = [Tile(0), Tile(1)]
    EPILOGUE = [Tile(t) for t in range(TILES - 2, TILES + 2)]

    x_view = x.rearrange("b (j s p) d -> b j p s d", s=SUB, p=P)
    out_view = out.rearrange("b (j s p) d -> b j s p d", s=SUB, p=P)

    ctx = ExitStack()
    with ctx:
        def sb(name, shape, dt=F32, where=ctx):
            return where.enter_context(nc.sbuf_tensor(name, shape, dt))

        def sem(name):
            return ctx.enter_context(nc.semaphore(name))

        HI, LO = 0, 1
        wq = [sb(f"wq{h}", [P, C, D], F32R) for h in range(2)]
        wo = [sb(f"wo{h}", [P, C, D], F32R) for h in range(2)]
        wf = [sb(f"wf{h}", [P, C, D], F32R) for h in range(2)]
        keys = sb("keys", [P, B, H // 2, 2, 2 * S], F32R)
        vals = sb("vals", [P, B, D])
        ident = sb("ident", [P, P])
        bo_row = sb("bo_row", [P, D])
        bf_row = sb("bf_row", [P, D])
        b_rows = sb("b_rows", [2 * C, P])
        b_cols = sb("b_cols", [P, 2 * C])
        bq_col, bk_col = b_cols[:, 0:C], b_cols[:, C:2 * C]
        minus_half = sb("minus_half", [P, SUB])
        neg_max = sb("neg_max", [P, 8, HG])
        den = sb("den", [P, 8, HG])
        rden = sb("rden", [P, 8, HG])
        st1 = sb("st1", [P, SUB, 6])
        mv1 = sb("mv1", [P, SUB, 2])
        ve1 = sb("ve1", [P, SUB])
        rstd1 = sb("rstd1", [P, SUB])
        st2 = sb("st2", [P, SUB, 6])
        mv2 = sb("mv2", [P, SUB, 2])
        ve2 = sb("ve2", [P, SUB])
        rstd2 = sb("rstd2", [P, SUB])

        x_sb = [sb(f"x_sb{j}", [P, SUB, D]) for j in range(2)]

        setup = ExitStack()
        with setup:
            ctx_t_hi = sb("ctx_t", [P, C, B * S], F32R, where=setup)
            wq_nat = sb("wq_nat", [P, C, D], where=setup)
            ctx_nat = sb("ctx_nat", [P, B, D], where=setup)
            wk_nat = sb("wk_nat", [P, C, D], where=setup)
            wk_t_hi = sb("wk_t", [P, C, D], F32R, where=setup)
            w0_nat = sb("w0_nat", [P, C, D], where=setup)
            w1_nat = sb("w1_nat", [P, C, D], where=setup)
            w2_nat = sb("w2_nat", [P, C, D], where=setup)
            wv_nat = sb("wv_nat", [P, C, D], where=setup)
        wo_nat = wv_nat
        setup_again = ExitStack()
        with setup_again:
            sb("below_wv_t", [P, C, D], where=setup_again)
            wv_t_hi = sb("wv_t", [P, C, D], F32R, where=setup_again)
            key_hi = sb("key_hi", [P, C, B * S], where=setup_again)
            key_lo = sb("key_lo", [P, C, B * S], where=setup_again)
            sb("below_w01_t", [P, C, D], where=setup_again)
            w01_t_hi = sb("w01_t", [P, C, D], F32R, where=setup_again)
            w1_lo = sb("w1_lo", [P, C, D], F32R, where=setup_again)
            w2_lo = sb("w2_lo", [P, C, D], F32R, where=setup_again)
            w1_hi = sb("w1_hi", [P, C, D], F32R, where=setup_again)

        split = {"ctx_t": (ctx_t_hi[:], wf[HI][:]), "wk_t": (wk_t_hi[:], wf[LO][:]), "wq_t": (wq[HI][:], wq[LO][:]),
                 "key": (key_hi[:].bitcast(F32R), key_lo[:].bitcast(F32R)), "wv_t": (wv_t_hi[:], wo[HI][:]), "w0_t": (wk_t_hi[:], wf[LO][:]),
                 "w1": (w1_hi[:], w1_lo[:]), "w01_t": (w01_t_hi[:], wo[HI][:]), "w2": (wo[LO][:], w2_lo[:]),
                 "wf": (wf[HI][:], wf[LO][:]), "wo_t": (wo[HI][:], wo[LO][:])}

        xn = sb("xn", [P, SUB, D])
        xn_t = [sb(f"xn_t{h}", [P, C, TOK], F32R) for h in range(2)]
        x_sb += [sb("x_sb2", [P, SUB, D])]
        q_st = sb("q_st", [P, C, 2, TOK], F32R)
        x_sb += [sb("x_sb3", [P, SUB, D])]
        probs = sb("probs", [P, 2, SUB, HG * S])
        probs_t = sb("probs_t", [P, 2, HG, TOK])
        work = sb("work", [P, SUB, D])
        ctx_o = [sb(f"ctx_o{h}", [P, 2, C, TOK], F32R) for h in range(2)]
        zn_t = [sb(f"zn_t{h}", [P, SUB, C, P], F32R) for h in range(2)]

        ps = ctx.enter_context(nc.psum_tensor("ps", [P, 8, 512], F32))

        consts = sem("consts")
        zeros = sem("zeros")
        L_CTX, L_WK, L_WQ, L_WV, L_W0, L_W1, L_W2, L_WO = (
            [sem(f"in_{n}{r}") for r in range(C)] for n in ("ctx", "wk", "wq", "wv", "w0", "w1", "w2", "wo"))
        L_QK = sem("in_bias_qk")
        L_V = sem("in_bias_v")
        L_B = sem("in_bias_rows")
        s_mm = sem("s_mm")
        s_act = sem("s_act")
        s_dve = sem("s_dve")
        s_split_hi = sem("s_split_hi")
        s_split_lo = sem("s_split_lo")
        s_key = sem("s_key")
        s_blocks = sem("s_blocks")
        x_in = [sem(f"x_in{j}") for j in range(UNROLL)]
        stored = [sem(f"stored{s}") for s in range(SUB)]
        scores_ready = sem("scores_ready")
        pt_ready = sem("pt_ready")
        ctx_ready = sem("ctx_ready")
        dense_ready = {F: sem("f_ready"), XT: sem("xt_ready"), Q: sem("q_ready"),
                       O: sem("o_ready"), Z0: sem("z0_ready"), Z1: sem("z1_ready")}
        exp_done = sem("exp_done")
        pt_act = sem("pt_act")
        pt_dve = sem("pt_dve")
        xn_hi = sem("xn_hi")
        q_hi = sem("q_hi")
        ctx_hi = sem("ctx_hi")
        zn_hi = [sem("zn_hi0"), sem("zn_hi1")]
        tanh_done = sem("tanh_done")
        max_done = sem("max_done")
        rden_done = sem("rden_done")
        xn_lo = sem("xn_lo")
        q_lo = sem("q_lo")
        ctx_lo = sem("ctx_lo")
        zn_lo = [sem("zn_lo0"), sem("zn_lo1")]
        arg_done = sem("arg_done")
        y_done = sem("y_done")
        mv1_done = sem("mv1_done")
        ve1_done = sem("ve1_done")
        mv2_done = sem("mv2_done")
        ve2_done = sem("ve2_done")
        xn_done = sem("xn_done")
        zn_done = sem("zn_done")
        rstd1_done = sem("rstd1_done")
        rstd2_done = sem("rstd2_done")
        xb_done = sem("xb_done")
        probs_ready = sem("probs_ready")
        out_done = sem("out_done")

        freed_by = {F: (arg_done, 2), XT: (xn_lo, 2), Q: (q_lo, 4), O: (y_done, 2), Z0: (zn_lo[0], 1),
                    Z1: (zn_lo[1], 1)}
        Z = [Z0, Z1]

        def wait(eng, semaphore, per_tile, tile, k):
            if tile.exists(TILES):
                eng.wait_ge(semaphore, count(per_tile, tile, k))

        def where(kind, n):
            return ps[:, BANK[kind, n], 0:TOK if kind == Q else D]

        sequence = []
        for item in ORD["pe"]:
            if len(item[0]) > 1 and (item[0], item[1]) not in sequence:
                sequence.append((item[0], item[1]))

        def last_user(t, kind, n):
            k = sequence.index((kind, n))
            for back in range(1, 3 * len(sequence)):
                other = sequence[(k - back) % len(sequence)]
                tile = t + (k - back) // len(sequence) + SHIFT[other[0]]
                if BANK[other] == BANK[kind, n] and tile.exists(TILES):
                    return (*other, tile)
            return None

        def four(name, how):
            return [(name, c, how[c % len(how)]) for c in range(C)]

        plan = ([("b_cols", 0, "d")] + four("ctx_t", ["ad"]) + four("wk_t", ["ad"]) + four("wq_t", ["ad"])
                + four("key", ["k"]) + four("wv_t", ["ad"]) + four("w0_t", ["ad"]) + four("val", ["d"]))
        ATTN = len(plan)
        plan += four("w01_t", ["ad"]) + four("wf", ["ad"]) + four("wo_t", ["ad"])
        names = [(name, c) for name, c, _ in plan]
        on_act = [how in ("ad", "k") for _, _, how in plan]
        on_dve = [how in ("d", "ad", "k") for _, _, how in plan]
        setup_bank = [m % 8 if m < ATTN else (m - ATTN) % 5 for m in range(len(plan))]
        TRANSPOSED = ("ctx_t", "wk_t", "wq_t", "wv_t", "w0_t", "wo_t")

        def placed(dst, name, c):
            return dst[:, :, c * P:(c + 1) * P] if name in TRANSPOSED else dst[:, c]

        def in_bank(m):
            bank = ps[:, setup_bank[m]]
            return bank.rearrange("p (k r) -> p k r", k=C) if names[m][0] in TRANSPOSED else bank

        def setup_copied(eng, m):
            if on_act[m]:
                eng.wait_ge(s_act, sum(on_act[:m + 1]))
            if on_dve[m]:
                eng.wait_ge(s_dve, sum(on_dve[:m + 1]))

        def setup_all(eng, name):
            for m in (names.index((name, 2)), names.index((name, 3))):
                setup_copied(eng, m)

        def products(*wanted, chunks=range(C)):
            return [m for m, (name, c) in enumerate(names) if name in wanted and c in chunks]

        EARLY = [k for name, shift, k in ORD["act"] if (name, shift) == ("q", 1)]

        def blocks_filled(eng):
            eng.wait_ge(s_blocks, 16 * C * HG * 4)

        block = ctx.enter_context(nc.Block())

        @block.sync
        def _(sp):
            def load_rows(dst, src, landed):
                for r in range(C):
                    sp.dma_start(dst[:, r], src[r * P:(r + 1) * P, :]).then_inc(landed[r], 16)

            def load(t):
                j = t.s // UNROLL if t.i is None else t.i + t.s // UNROLL
                sp.dma_start(x_sb[t.s % UNROLL][:], x_view[t.s % B, j]).then_inc(x_in[t.s % UNROLL], 16)

            load_rows(ctx_nat, ctx_in.rearrange("b s d -> (b s) d"), L_CTX)
            load_rows(wk_nat, w_in[D:2 * D, :], L_WK)
            load_rows(wq_nat, w_in[0:D, :], L_WQ)
            load_rows(wv_nat, w_in[2 * D:3 * D, :], L_WV)
            for t in range(2):
                load(Tile(t))
            load_rows(w0_nat, w_ffn, L_W0)
            load_rows(w1_nat, w_aux1, L_W1)
            load_rows(w2_nat, w_aux2, L_W2)

            sp.wait_ge(zeros, 2)
            for c in range(C):
                setup_copied(sp, names.index(("key", c)))
                for j in range(HG):
                    pair, h = 2 * c + j // 2, j % 2
                    for half, kc in ((HI, key_hi), (LO, key_lo)):
                        for row in (HD * h, P // 2 + HD * h):
                            sp.dma_start(
                                keys[row:row + HD, :, pair, half, h * S:(h + 1) * S].bitcast(F32),
                                kc[HD * j:HD * (j + 1), c, :].rearrange("p (b s) -> p b s", b=B),
                            ).then_inc(s_blocks, 16)

            sp.wait_ge(s_mm, products("val")[-1] + 1)
            blocks_filled(sp)
            for t in range(2, UNROLL):
                load(Tile(t))
            sp.wait_ge(s_mm, products("w01_t")[-1] + 1)
            load_rows(wo_nat, w_out, L_WO)

            def iteration(t):
                done, more = t - 2, t + 2
                for s in range(SUB):
                    if done.exists(TILES):
                        wait(sp, out_done, 2, done, s)
                        j = done.s // UNROLL if t.i is None else t.i + done.s // UNROLL
                        sp.dma_start(out_view[done.s % B, j, s], work[:, s]).then_inc(stored[s], 16)
                if done.exists(TILES) and more.exists(TILES):
                    load(more)

            for t in PROLOGUE:
                iteration(t)
            with sp.Fori(0, LOOPS) as i:
                for k in range(UNROLL):
                    iteration(Tile(2 + k, i))
            for t in EPILOGUE:
                iteration(t)
            for s in range(SUB):
                sp.wait_ge(stored[s], 16 * TILES)

        @block.gpsimd
        def _(pool):
            nc.gpsimd.memset(ident[:], 0.0).then_inc(consts, 1)
            nc.gpsimd.memset(minus_half[:], -0.5).then_inc(consts, 1)
            pool.wait_ge(consts, 2)
            nc.gpsimd.affine_select(out=ident[:], in_=ident[:], compare_op=ALU.not_equal, fill=1.0, base=0,
                                    pattern=[[-1, P]], channel_multiplier=1).then_inc(consts, 1)
            for h in range(2):
                nc.gpsimd.memset(keys[:, h * B // 2:(h + 1) * B // 2].bitcast(F32), 0.0).then_inc(zeros, 1)
            pool.wait_ge(L_B, 16 * 2)

            def normalise_probs(t, n):
                g, s = n // 2, n % 2
                if not t.exists(TILES):
                    return
                wait(pool, rden_done, 8, t, n)
                pr = probs[:, g % 2, s].rearrange("p (h k) -> p h k", h=HG)
                nc.gpsimd.tensor_tensor(pr, pr, rden[:, n].unsqueeze(2).to_broadcast([P, HG, S]),
                                        ALU.mult).then_inc(probs_ready, 1)

            def add_bias(t, s):
                if t.exists(TILES):
                    wait(pool, xn_done, 2, t, s)
                    xs = x_sb[t.s % UNROLL][:, s]
                    nc.gpsimd.tensor_tensor(xs, xs, bo_row[:], ALU.add).then_inc(xb_done, 1)

            def result(t, s):
                if t.exists(TILES):
                    wait(pool, tanh_done, 2, t, s)
                    nc.gpsimd.tensor_tensor(work[:, s], work[:, s], x_sb[t.s % UNROLL][:, s],
                                            ALU.add).then_inc(out_done, 1)

            def y_rstd(t, s):
                if t.exists(TILES):
                    wait(pool, ve2_done, 2, t, s)
                    nc.gpsimd.tensor_tensor(rstd2[:, s:s + 1], ve2[:, s:s + 1], minus_half[:, 0:1],
                                            ALU.pow).then_inc(rstd2_done, 1)

            def x_rstd(t, s):
                if t.exists(TILES):
                    wait(pool, ve1_done, 1, t, 0)
                    nc.gpsimd.tensor_tensor(rstd1[:], ve1[:], minus_half[:], ALU.pow).then_inc(rstd1_done, 1)

            def iteration(t):
                fs = dict(norm=normalise_probs, bias=add_bias, res=result, yr=y_rstd, xr=x_rstd)
                for name, shift, k in ORD["pool"]:
                    fs[name](t + shift, k)

            x_rstd(Tile(0), 0)
            for s in range(SUB):
                add_bias(Tile(0), s)
            x_rstd(Tile(1), 0)
            for t in PROLOGUE:
                iteration(t)
            with pool.Fori(0, LOOPS) as i:
                for k in range(UNROLL):
                    iteration(Tile(2 + k, i))
            for t in EPILOGUE:
                iteration(t)

        @block.scalar
        def _(act):
            act.dma_start(b_rows[:], b_in[0:2 * D].rearrange("(c p) -> c p", p=P)).then_inc(L_QK, 16)
            act.dma_start(vals[:, B - 1], b_in[2 * D:3 * D].partition_broadcast(P)).then_inc(L_V, 16)
            act.dma_start(bo_row[:], b_out.partition_broadcast(P)).then_inc(L_B, 16)
            act.dma_start(bf_row[:], b_ffn.partition_broadcast(P)).then_inc(L_B, 16)

            def setup_copy(*names_wanted, chunks=range(C)):
                for m in products(*names_wanted, chunks=chunks):
                    name, c, how = plan[m]
                    if not on_act[m]:
                        continue
                    act.wait_ge(s_mm, m + 1)
                    if name == "key":
                        act.wait_ge(s_key, c + 1)
                    nc.scalar.copy(placed(split[name][HI], name, c), in_bank(m)).then_inc(s_act, 1)

            def setup_split(name, nat, landed):
                for c in range(C):
                    act.wait_ge(landed[c], 16)
                    nc.scalar.copy(split[name][HI][:, c], nat[:, c]).then_inc(s_split_hi, 1)

            def exps(t, n):
                g, s = n // 2, n % 2
                if not t.exists(TILES):
                    return
                wait(act, max_done, 8, t, n)
                wait(act, pt_ready, 8, t if g >= 2 else t - 1, 2 * g - 3 if g >= 2 else 2 * g + 5)
                for h in range(HG):
                    last = nc.scalar.activation(probs[:, g % 2, s, h * S:(h + 1) * S],
                                                ps[:, n % 2, h * S:(h + 1) * S], ACT.Exp,
                                                bias=neg_max[:, n, h:h + 1], accum_out=den[:, n, h:h + 1])
                last.then_inc(exp_done, 1)

            def copy_probs_t(t, idx):
                g = idx // 2
                if t.exists(TILES):
                    wait(act, pt_ready, 8, t, idx)
                    wait(act, ctx_ready, 4, t if g >= 2 else t - 1, (g - 2) % 4)
                    nc.scalar.copy(probs_t[:, g % 2, 2:4].rearrange("p h t -> p (h t)"),
                                   ps[:, 2 + idx % 2]).then_inc(pt_act, 1)

            def context_hi(t, g):
                if t.exists(TILES):
                    wait(act, ctx_ready, 4, t, g)
                    wait(act, dense_ready[O], 2, t - 2, 1)
                    nc.scalar.copy(ctx_o[HI][:, t.s % 2, g], ps[:, CTX_BANK, 0:TOK]).then_inc(ctx_hi, 1)

            def xn_t_hi(t, s):
                if t.exists(TILES):
                    wait(act, dense_ready[XT], 2, t, s)
                    wait(act, dense_ready[Q], 4, t - 1, C - 1)
                    nc.scalar.copy(xn_t[HI][:, :, s * P:(s + 1) * P],
                                   where(XT, s).rearrange("p (c t) -> p c t", c=C)).then_inc(xn_hi, 1)

            def query_hi(t, c):
                if t.exists(TILES):
                    wait(act, dense_ready[Q], 4, t, c)
                    wait(act, scores_ready, 8, t - 1, 2 * c + 1)
                    for pair in range(2):
                        rows = slice(pair * P // 2, (pair + 1) * P // 2)
                        last = nc.scalar.activation(q_st[rows, c, pair], where(Q, c)[rows],
                                                    ACT.Identity, bias=bq_col[rows, c:c + 1])
                    last.then_inc(q_hi, 1)

            def z_t_hi(t, s):
                if t.exists(TILES):
                    wait(act, dense_ready[Z[s]], 1, t, 0)
                    wait(act, dense_ready[F], 2, t - 1, s)
                    nc.scalar.copy(zn_t[HI][:, s].rearrange("p c t -> p (c t)"),
                                   where(Z[s], 0)).then_inc(zn_hi[s], 1)

            def tanh(t, s):
                if t.exists(TILES):
                    wait(act, arg_done, 2, t, s)
                    nc.scalar.activation(work[:, s], work[:, s], ACT.Tanh).then_inc(tanh_done, 1)

            def iteration(t):
                fs = dict(exp=exps, pt=copy_probs_t, ctx=context_hi, xt=xn_t_hi, q=query_hi, z=z_t_hi, tanh=tanh)
                for name, shift, k in ORD["act"]:
                    fs[name](t + shift, k)

            setup_copy("ctx_t", "wk_t", "wq_t", "key", "wv_t", "w0_t")
            setup_split("w1", w1_nat, L_W1)
            setup_split("w2", w2_nat, L_W2)
            setup_copy("w01_t", chunks=range(2))
            xn_t_hi(Tile(0), 0)
            setup_copy("w01_t", chunks=[2])
            xn_t_hi(Tile(0), 1)
            setup_copy("w01_t", chunks=[3])
            setup_copy("wf", chunks=range(3))
            blocks_filled(act)
            for c in EARLY:
                if c == 2:
                    setup_copy("wf", chunks=[3])
                    setup_copy("wo_t")
                query_hi(Tile(0), c)
            for t in PROLOGUE:
                iteration(t)
            with act.Fori(0, LOOPS) as i:
                for k in range(UNROLL):
                    iteration(Tile(2 + k, i))
            for t in EPILOGUE:
                iteration(t)

        @block.vector
        def _(dve):
            dve.wait_ge(L_V, 16)
            dve.wait_ge(L_B, 16 * 2)
            def setup_copy(*names_wanted, chunks=range(C)):
                for m in products(*names_wanted, chunks=chunks):
                    name, c, how = plan[m]
                    if not on_dve[m]:
                        continue
                    dve.wait_ge(s_mm, m + 1)
                    bank = in_bank(m)
                    if name == "key":
                        nc.vector.tensor_scalar(bank, bank, bk_col[:, c:c + 1], SCALE,
                                                ALU.add, ALU.mult).then_inc(s_key, 1)
                        dve.wait_ge(s_key, c + 1)
                    if how in ("ad", "k"):
                        dve.wait_ge(s_act, sum(on_act[:m + 1]))
                        hi, lo = (placed(half, name, c) for half in split[name])
                        nc.vector.tensor_tensor(lo, bank, hi.bitcast(F32), ALU.subtract).then_inc(s_dve, 1)
                    elif name == "val":
                        nc.vector.tensor_tensor(vals[:, c], bank, vals[:, B - 1], ALU.add).then_inc(s_dve, 1)
                    else:
                        nc.vector.tensor_copy(b_cols[:], bank[:, 0:2 * C]).then_inc(s_dve, 1)
                        dve.wait_ge(s_dve, 1)

            def setup_split(name, nat, done):
                for c in range(C):
                    dve.wait_ge(s_split_hi, done + c + 1)
                    nc.vector.tensor_tensor(split[name][LO][:, c], nat[:, c], split[name][HI][:, c].bitcast(F32),
                                            ALU.subtract).then_inc(s_split_lo, 1)

            def maxima(t, n):
                if not t.exists(TILES):
                    return
                wait(dve, scores_ready, 8, t, n)
                nc.vector.tensor_reduce(neg_max[:, n], ps[:, n % 2].rearrange("p (h k) -> p h k", h=HG),
                                        AX.X, ALU.max, negate=True).then_inc(max_done, 1)

            def reciprocals(t, n):
                if not t.exists(TILES):
                    return
                wait(dve, exp_done, 8, t, n)
                nc.vector.reciprocal(rden[:, n], den[:, n]).then_inc(rden_done, 1)

            def copy_probs_t(t, idx):
                g = idx // 2
                if t.exists(TILES):
                    wait(dve, pt_ready, 8, t, idx)
                    wait(dve, ctx_ready, 4, t if g >= 2 else t - 1, (g - 2) % 4)
                    nc.vector.tensor_copy(probs_t[:, g % 2, 0:2].rearrange("p h t -> p (h t)"),
                                          ps[:, 2 + idx % 2]).then_inc(pt_dve, 1)

            def context_lo(t, g):
                if t.exists(TILES):
                    wait(dve, ctx_hi, 4, t, g)
                    nc.vector.tensor_tensor(ctx_o[LO][:, t.s % 2, g], ps[:, CTX_BANK, 0:TOK],
                                            ctx_o[HI][:, t.s % 2, g].bitcast(F32), ALU.subtract).then_inc(ctx_lo, 1)

            def xn_t_lo(t, s):
                if t.exists(TILES):
                    wait(dve, xn_hi, 2, t, s)
                    cols = slice(s * P, (s + 1) * P)
                    nc.vector.tensor_tensor(xn_t[LO][:, :, cols],
                                            where(XT, s).rearrange("p (c t) -> p c t", c=C),
                                            xn_t[HI][:, :, cols].bitcast(F32), ALU.subtract).then_inc(xn_lo, 1)

            def query_lo(t, c):
                if t.exists(TILES):
                    wait(dve, q_hi, 4, t, c)
                    for pair in range(2):
                        rows = slice(pair * P // 2, (pair + 1) * P // 2)
                        other = slice((1 - pair) * P // 2, (2 - pair) * P // 2)
                        last = nc.vector.scalar_tensor_tensor(
                            out=q_st[other, c, pair], in0=where(Q, c)[rows],
                            scalar=bq_col[rows, c:c + 1], in1=q_st[rows, c, pair].bitcast(F32),
                            op0=ALU.add, op1=ALU.subtract)
                    last.then_inc(q_lo, 1)

            def z_t_lo(t, s):
                if t.exists(TILES):
                    wait(dve, zn_hi[s], 1, t, 0)
                    nc.vector.tensor_tensor(zn_t[LO][:, s].rearrange("p c t -> p (c t)"), where(Z[s], 0),
                                            zn_t[HI][:, s].rearrange("p c t -> p (c t)").bitcast(F32),
                                            ALU.subtract).then_inc(zn_lo[s], 1)

            def tanh_argument(t, s):
                if t.exists(TILES):
                    wait(dve, dense_ready[F], 2, t, s)
                    nc.vector.tensor_tensor(work[:, s], where(F, s), bf_row[:], ALU.add).then_inc(arg_done, 1)

            def x_statistics(t, k=0):
                if t.exists(TILES):
                    slot = t.s % UNROLL
                    turns = t.s // UNROLL + 1 if t.i is None else t.i + (t.s // UNROLL + 1)
                    dve.wait_ge(x_in[slot], turns * 16)
                    wait(dve, rstd1_done, 1, t - 1, 0)
                    for s in range(SUB):
                        nc.vector.bn_stats(st1[:, s], x_sb[slot][:, s])
                    nc.vector.drain()
                    for s in range(SUB):
                        nc.vector.bn_aggr(mv1[:, s], st1[:, s]).then_inc(mv1_done, 1)
                    wait(dve, mv1_done, 2, t, 1)
                    nc.vector.tensor_scalar_add(ve1[:], mv1[:, :, 1], EPS).then_inc(ve1_done, 1)

            def x_normalise(t, s):
                if t.exists(TILES):
                    wait(dve, rstd1_done, 1, t, 0)
                    wait(dve, dense_ready[XT], 2, t - 1, s)
                    nc.vector.tensor_scalar(xn[:, s], x_sb[t.s % UNROLL][:, s], mv1[:, s, 0:1],
                                            rstd1[:, s:s + 1], ALU.subtract, ALU.mult).then_inc(xn_done, 1)

            def residual(t, s):
                if t.exists(TILES):
                    xs = x_sb[t.s % UNROLL][:, s]
                    wait(dve, dense_ready[O], 2, t, s)
                    wait(dve, xb_done, 2, t, s)
                    nc.vector.tensor_tensor(xs, where(O, s), xs, ALU.add).then_inc(y_done, 1)
                    wait(dve, y_done, 2, t, s)
                    nc.vector.bn_stats(st2[:, s], xs)

            def y_statistics(t, s):
                if t.exists(TILES):
                    nc.vector.drain()
                    nc.vector.bn_aggr(mv2[:, s], st2[:, s]).then_inc(mv2_done, 1)
                    wait(dve, mv2_done, 2, t, s)
                    nc.vector.tensor_scalar_add(ve2[:, s:s + 1], mv2[:, s, 1:2], EPS).then_inc(ve2_done, 1)

            def y_normalise(t, s):
                if t.exists(TILES):
                    wait(dve, rstd2_done, 2, t, s)
                    if (t - 1).exists(TILES):
                        dve.wait_ge(stored[s], 16 * t.s if t.i is None else t.i * (16 * UNROLL) + 16 * t.s)
                    nc.vector.tensor_scalar(work[:, s], x_sb[t.s % UNROLL][:, s], mv2[:, s, 0:1],
                                            rstd2[:, s:s + 1], ALU.subtract, ALU.mult).then_inc(zn_done, 1)

            def iteration(t):
                fs = dict(max=maxima, rec=reciprocals, pt=copy_probs_t, ctx=context_lo, xt=xn_t_lo, q=query_lo,
                          z=z_t_lo, arg=tanh_argument, xs=x_statistics, xn=x_normalise, y=residual,
                          ys=y_statistics, yn=y_normalise)
                for name, shift, k in ORD["dve"]:
                    fs[name](t + shift, k)

            setup_copy("b_cols", "ctx_t", "wk_t", "wq_t", "key", "wv_t", "w0_t")
            x_statistics(Tile(0))
            setup_split("w1", w1_nat, 0)
            setup_copy("val")
            for s in range(SUB):
                x_normalise(Tile(0), s)
            setup_split("w2", w2_nat, C)
            setup_copy("w01_t", chunks=range(2))
            xn_t_lo(Tile(0), 0)
            setup_copy("w01_t", chunks=[2])
            xn_t_lo(Tile(0), 1)
            setup_copy("w01_t", chunks=[3])
            x_statistics(Tile(1))
            setup_copy("wf", chunks=[0])
            for s in range(SUB):
                x_normalise(Tile(1), s)
            setup_copy("wf", chunks=range(1, 3))
            for c in EARLY:
                if c == 2:
                    setup_copy("wf", chunks=[3])
                    setup_copy("wo_t")
                query_lo(Tile(0), c)
            for t in PROLOGUE:
                iteration(t)
            with dve.Fori(0, LOOPS) as i:
                for k in range(UNROLL):
                    iteration(Tile(2 + k, i))
            for t in EPILOGUE:
                iteration(t)

        @block.tensor
        def _(pe):
            pe.wait_ge(consts, 3)
            nat = {"ctx_t": (ctx_nat, L_CTX), "wk_t": (wk_nat, L_WK), "wq_t": (wq_nat, L_WQ),
                   "wv_t": (wv_nat, L_WV), "w0_t": (w0_nat, L_W0), "wo_t": (wo_nat, L_WO)}

            PASSES = [(half, k) for half in ((HI, HI), (LO, HI), (HI, LO)) for k in range(C)]

            def product(bank, lhs_t, cols, rhs):
                for j, ((a, b), k) in enumerate(PASSES):
                    last = nc.tensor.matmul(bank, split[lhs_t][a][:, k, cols], split[rhs][b][:, k],
                                            start=(j == 0), stop=(j == len(PASSES) - 1))
                return last

            def setup_products(*names_wanted, chunks=range(C)):
                for m in products(*names_wanted, chunks=chunks):
                    last = setup_product(m)
                    last.then_inc(s_mm, 1)

            def setup_product(m):
                name, c, how = plan[m]
                bank = ps[:, setup_bank[m]]
                if setup_bank[m] in setup_bank[:m]:
                    setup_copied(pe, max(k for k in range(m) if setup_bank[k] == setup_bank[m]))
                cols = slice(c * P, (c + 1) * P)
                if name == "b_cols":
                    pe.wait_ge(L_QK, 16)
                    return nc.tensor.transpose(bank[:, 0:2 * C], b_rows[:], ident[0:2 * C, 0:2 * C])
                if name in nat:
                    src, landed = nat[name]
                    pe.wait_ge(landed[c], 16)
                    for k in range(C):
                        last = nc.tensor.transpose(bank[:, k * P:(k + 1) * P], src[:, c, k * P:(k + 1) * P], ident[:])
                    return last
                if name == "key":
                    if c == 0:
                        setup_all(pe, "ctx_t")
                        setup_all(pe, "wk_t")
                    return product(bank, "wk_t", cols, "ctx_t")
                if name == "val":
                    if c == 0:
                        setup_all(pe, "wv_t")
                    return product(bank, "ctx_t", cols, "wv_t")
                if name == "w01_t":
                    if c == 0:
                        pe.wait_ge(s_split_lo, C)
                        setup_all(pe, "w0_t")
                    return product(bank, "w1", cols, "w0_t")
                if c == 0:
                    pe.wait_ge(s_split_lo, 2 * C)
                    setup_all(pe, "w01_t")
                return product(bank, "w01_t", cols, "w2")

            def scores(t, n):
                g, s = n // 2, n % 2
                if not t.exists(TILES):
                    return
                wait(pe, q_lo, 4, t, g)
                wait(pe, exp_done, 8, t if n >= 2 else t - 1, (n - 2) % 8)
                for pair in range(2):
                    for half in (HI, LO):
                        last = nc.tensor.matmul(ps[:, n % 2, pair * 2 * S:(pair + 1) * 2 * S],
                                                q_st[:, g, pair, s * P:(s + 1) * P],
                                                keys[:, t.s % B, 2 * g + pair, half],
                                                start=(half == HI), stop=(half == LO))
                last.then_inc(scores_ready, 1)

            def transpose_probs(t, idx):
                if not t.exists(TILES):
                    return
                g, pair = idx // 2, idx % 2
                wait(pe, probs_ready, 8, t, 2 * g + 1)
                wait(pe, pt_dve if idx % 2 == 0 else pt_act, 4, t if g else t - 1, (g - 1) % 4)
                for h in range(2):
                    for s in range(SUB):
                        col = (2 * pair + h) * S
                        last = nc.tensor.transpose(ps[:, 2 + idx % 2, (h * SUB + s) * P:(h * SUB + s + 1) * P],
                                                   probs[:, g % 2, s, col:col + S], ident[:])
                last.then_inc(pt_ready, 1)

            def context(t, g):
                if not t.exists(TILES):
                    return
                wait(pe, pt_dve, 4, t, g)
                wait(pe, pt_act, 4, t, g)
                wait(pe, ctx_lo, 4, t if g else t - 1, (g - 1) % 4)
                for h in range(HG):
                    f = (g * HG + h) * HD
                    last = nc.tensor.matmul(ps[HD * h:HD * (h + 1), CTX_BANK, 0:TOK],
                                            vals[:, t.s % B, f:f + HD], probs_t[:, g % 2, h],
                                            start=True, stop=True, tile_position=(0, HD * h))
                last.then_inc(ctx_ready, 1)

            def dense(t_iter, kind, n, part):
                t = t_iter + SHIFT[kind]
                if not t.exists(TILES):
                    return
                bank = where(kind, n)
                if part == 0:
                    before = last_user(t_iter, kind, n)
                    if before:
                        freed, per_tile = freed_by[before[0]]
                        wait(pe, freed, per_tile, before[2], before[1])
                if kind in (XT, Z0, Z1):
                    half = {XT: n, Z0: 0, Z1: 1}[kind]
                    src, ready = (xn, xn_done) if kind == XT else (work, zn_done)
                    wait(pe, ready, 2, t, half)
                    for c in range(C):
                        last = nc.tensor.transpose(bank[:, c * P:(c + 1) * P], src[:, half, c * P:(c + 1) * P], ident[:])
                    last.then_inc(dense_ready[kind], 1)
                    return
                if kind == Q:
                    if part == 0:
                        wait(pe, xn_lo, 2, t, 1)
                    dst = bank
                elif kind == O:
                    if part == 0:
                        wait(pe, ctx_lo, 4, t, C - 1)
                    dst = bank
                else:
                    if part == 0:
                        wait(pe, zn_lo[n], 1, t, 0)
                    dst = bank
                size = len(PASSES) // PARTS[kind]
                for j in range(part * size, (part + 1) * size):
                    (a, w), k = PASSES[j]
                    if kind == Q:
                        lhs, rhs = wq[w][:, k, n * P:(n + 1) * P], xn_t[a][:, k]
                    elif kind == O:
                        lhs, rhs = ctx_o[a][:, t.s % 2, k, n * P:(n + 1) * P], wo[w][:, k]
                    else:
                        lhs, rhs = zn_t[a][:, n, k], wf[w][:, k]
                    last = nc.tensor.matmul(dst, lhs, rhs, start=(j == 0), stop=(j == len(PASSES) - 1))
                if part == PARTS[kind] - 1:
                    last.then_inc(dense_ready[kind], 1)

            def iteration(t):
                fs = dict(S=scores, T=transpose_probs, C=context)
                for item in ORD["pe"]:
                    if item[0] in fs:
                        fs[item[0]](t + item[1], item[2])
                    else:
                        dense(t, *item)

            setup_products("b_cols", "ctx_t", "wk_t", "wq_t", "key", "wv_t", "w0_t", "val")
            setup_products("w01_t", chunks=range(2))
            setup_copied(pe, ATTN - 1)
            dense(Tile(-1), XT, 0, 0)
            setup_products("w01_t", chunks=[2])
            dense(Tile(-1), XT, 1, 0)
            setup_products("w01_t", chunks=[3])
            setup_products("wf", chunks=range(3))
            for c in range(C):
                if c == 2:
                    setup_products("wf", chunks=[3])
                    setup_products("wo_t")
                for part in range(PARTS[Q]):
                    dense(Tile(-1), Q, c, part)
            setup_copied(pe, len(plan) - 1)
            blocks_filled(pe)
            for t in PROLOGUE:
                iteration(t)
            with pe.Fori(0, LOOPS) as i:
                for k in range(UNROLL):
                    iteration(Tile(2 + k, i))
            for t in EPILOGUE:
                iteration(t)


_INS = ["x", "ctx_1024", "L0_xattn_in_proj_weight", "L0_xattn_in_proj_bias", "L0_xattn_out_w", "L0_xattn_out_b",
        "L0_ffn_weight", "L0_ffn_aux_weight1", "L0_ffn_aux_weight2", "L0_ffn_bias"]


def kernel(**inputs):
    import numpy as _np
    import concourse.bacc as _bacc
    from concourse import mybir as _mybir
    from concourse.bass_utils import run_bass_kernel_spmd as _run

    nc = _bacc.Bacc("TRN2", target_bir_lowering=False, num_devices=1)
    arrays, args = {}, []
    for name in _INS:
        a = _np.ascontiguousarray(inputs[name])
        arrays[f"in_{name}"] = a
        args.append(nc.dram_tensor(f"in_{name}", a.shape, _mybir.dt.from_np(a.dtype), kind="ExternalInput").ap())
    shape = inputs["x"].shape
    args.append(nc.dram_tensor("out_y", shape, _mybir.dt.float32, kind="ExternalOutput").ap())
    build(nc, *args)
    r = _run(nc, [arrays], core_ids=[0])
    return r.results[0]["out_y"]
```

```python
from contextlib import ExitStack

import concourse.bass as bass
from concourse import mybir

F32 = mybir.dt.float32
F32R = mybir.dt.float32r
ACT = mybir.ActivationFunctionType
ALU = mybir.AluOpType
AX = mybir.AxisListType

P = 128
D = 512
C = D // P
H = 16
HD = D // H
HG = P // HD
SUB = 2
TOK = SUB * P
UNROLL = 4
EPS = 1e-5


class Tile:

    def __init__(self, s, i=None):
        self.s, self.i = s, i

    def __add__(self, d):
        return Tile(self.s + d, self.i)

    def __sub__(self, d):
        return Tile(self.s - d, self.i)

    def exists(self, tiles):
        return self.i is not None or 0 <= self.s < tiles


def count(per_tile, tile, k):
    if tile.i is None:
        return per_tile * tile.s + k + 1
    return tile.i * (UNROLL * per_tile) + (per_tile * tile.s + k + 1)


F, XT, Q, O, Z0, Z1 = "ffn", "xn transpose", "query", "out", "z transpose 0", "z transpose 1"
PARTS = {F: 4, XT: 1, Q: 2, O: 4, Z0: 1, Z1: 1}
CTX_BANK = 4
DENSE = [(F, 0, 5), (Z1, 0, 6), (F, 1, 6), (XT, 0, 7), (XT, 1, 5), (Q, 0, 7), (O, 0, 6), (Q, 1, 6),
         (O, 1, 7), (Q, 2, 6), (Z0, 0, 5), (Q, 3, 7)]
BANK = {(kind, n): bank for kind, n, bank in DENSE}
SEQUENCE = [(kind, n) for kind, n, _ in DENSE]
SHIFT = {F: -2, XT: 1, Q: 1, O: -1, Z0: -1, Z1: -2}


def build(nc, x, ctx_in, w_in, b_in, w_out, b_out, w_ffn, w_aux1, w_aux2, b_ffn, out):
    B, T, _ = x.shape
    S = ctx_in.shape[1]
    TILES = B * T // TOK
    SCALE = float(HD) ** -0.5
    assert S == P and x.shape[2] == D and UNROLL == B and (TILES - 4) % UNROLL == 0
    LOOPS = (TILES - 4) // UNROLL
    PROLOGUE = [Tile(0), Tile(1)]
    EPILOGUE = [Tile(t) for t in range(TILES - 2, TILES + 2)]

    x_view = x.rearrange("b (j s p) d -> b j p s d", s=SUB, p=P)
    out_view = out.rearrange("b (j s p) d -> b j s p d", s=SUB, p=P)

    ctx = ExitStack()
    with ctx:
        def sb(name, shape, dt=F32, where=ctx):
            return where.enter_context(nc.sbuf_tensor(name, shape, dt))

        def sem(name):
            return ctx.enter_context(nc.semaphore(name))

        HI, LO = 0, 1
        wq = [sb(f"wq{h}", [P, C, D], F32R) for h in range(2)]
        wo = [sb(f"wo{h}", [P, C, D], F32R) for h in range(2)]
        wf = [sb(f"wf{h}", [P, C, D], F32R) for h in range(2)]
        keys = sb("keys", [P, 2, 2, C, B, 2 * S], F32R)
        vals = sb("vals", [P, B, D])
        ident = sb("ident", [P, P])
        bo_row = sb("bo_row", [P, D])
        bf_row = sb("bf_row", [P, D])
        b_rows = sb("b_rows", [2 * C, P])
        b_cols = sb("b_cols", [P, 2 * C])
        bq_col, bk_col = b_cols[:, 0:C], b_cols[:, C:2 * C]
        minus_half = sb("minus_half", [P, SUB])
        neg_max = sb("neg_max", [P, 8, HG])
        den = sb("den", [P, 8, HG])
        rden = sb("rden", [P, 8, HG])
        st1 = sb("st1", [P, SUB, 6])
        mv1 = sb("mv1", [P, SUB, 2])
        ve1 = sb("ve1", [P, SUB])
        rstd1 = sb("rstd1", [P, SUB])
        st2 = sb("st2", [P, SUB, 6])
        mv2 = sb("mv2", [P, SUB, 2])
        ve2 = sb("ve2", [P, SUB])
        rstd2 = sb("rstd2", [P, SUB])

        x_sb = [sb(f"x_sb{j}", [P, SUB, D]) for j in range(2)]

        setup = ExitStack()
        with setup:
            ctx_t_hi = sb("ctx_t", [P, C, B * S], F32R, where=setup)
            wq_nat = sb("wq_nat", [P, C, D], where=setup)
            ctx_nat = sb("ctx_nat", [P, B, D], where=setup)
            wk_nat = sb("wk_nat", [P, C, D], where=setup)
            wk_t_hi = sb("wk_t", [P, C, D], F32R, where=setup)
            w0_nat = sb("w0_nat", [P, C, D], where=setup)
            w1_nat = sb("w1_nat", [P, C, D], where=setup)
            w2_nat = sb("w2_nat", [P, C, D], where=setup)
            wv_nat = sb("wv_nat", [P, C, D], where=setup)
        wo_nat = wv_nat
        setup_again = ExitStack()
        with setup_again:
            sb("below_wv_t", [P, C, D], where=setup_again)
            wv_t_hi = sb("wv_t", [P, C, D], F32R, where=setup_again)
            key_hi = sb("key_hi", [P, C, B * S], where=setup_again)
            key_lo = sb("key_lo", [P, C, B * S], where=setup_again)
            sb("below_w01_t", [P, C, D], where=setup_again)
            w01_t_hi = sb("w01_t", [P, C, D], F32R, where=setup_again)
            w1_lo = sb("w1_lo", [P, C, D], F32R, where=setup_again)
            w2_lo = sb("w2_lo", [P, C, D], F32R, where=setup_again)
            w1_hi = sb("w1_hi", [P, C, D], F32R, where=setup_again)

        split = {"ctx_t": (ctx_t_hi[:], wf[HI][:]), "wk_t": (wk_t_hi[:], wf[LO][:]), "wq_t": (wq[HI][:], wq[LO][:]),
                 "key": (key_hi[:].bitcast(F32R), key_lo[:].bitcast(F32R)),
                 "wv_t": (wv_t_hi[:], wo[HI][:]), "w0_t": (wk_t_hi[:], wf[LO][:]),
                 "w1": (w1_hi[:], w1_lo[:]), "w01_t": (w01_t_hi[:], wo[HI][:]), "w2": (wo[LO][:], w2_lo[:]),
                 "wf": (wf[HI][:], wf[LO][:]), "wo_t": (wo[HI][:], wo[LO][:])}

        xn = sb("xn", [P, SUB, D])
        xn_t = [sb(f"xn_t{h}", [P, C, TOK], F32R) for h in range(2)]
        x_sb += [sb("x_sb2", [P, SUB, D])]
        q_st = sb("q_st", [P, C, 2, TOK], F32R)
        x_sb += [sb("x_sb3", [P, SUB, D])]
        probs = sb("probs", [P, 2, SUB, HG * S])
        probs_t = sb("probs_t", [P, 2, HG, TOK])
        work = sb("work", [P, SUB, D])
        ctx_o = [sb(f"ctx_o{h}", [P, 2, C, TOK], F32R) for h in range(2)]
        zn_t = [sb(f"zn_t{h}", [P, SUB, C, P], F32R) for h in range(2)]

        ps = ctx.enter_context(nc.psum_tensor("ps", [P, 8, 512], F32))

        consts = sem("consts")
        zeros = sem("zeros")
        L_CTX, L_WK, L_WQ, L_WV, L_W0, L_W1, L_W2, L_WO = (
            [sem(f"in_{n}{r}") for r in range(C)] for n in ("ctx", "wk", "wq", "wv", "w0", "w1", "w2", "wo"))
        L_QK = sem("in_bias_qk")
        L_V = sem("in_bias_v")
        L_B = sem("in_bias_rows")
        s_mm = sem("s_mm")
        s_act = sem("s_act")
        s_dve = sem("s_dve")
        s_split_hi = sem("s_split_hi")
        s_split_lo = sem("s_split_lo")
        s_key = sem("s_key")
        s_blocks = sem("s_blocks")
        x_in = [sem(f"x_in{j}") for j in range(UNROLL)]
        stored = [sem(f"stored{s}") for s in range(SUB)]
        scores_ready = sem("scores_ready")
        pt_ready = sem("pt_ready")
        ctx_ready = sem("ctx_ready")
        dense_ready = {F: sem("f_ready"), XT: sem("xt_ready"), Q: sem("q_ready"),
                       O: sem("o_ready"), Z0: sem("z0_ready"), Z1: sem("z1_ready")}
        exp_done = sem("exp_done")
        pt_act = sem("pt_act")
        pt_dve = sem("pt_dve")
        xn_hi = sem("xn_hi")
        q_hi = sem("q_hi")
        ctx_hi = sem("ctx_hi")
        zn_hi = [sem("zn_hi0"), sem("zn_hi1")]
        tanh_done = sem("tanh_done")
        max_done = sem("max_done")
        rden_done = sem("rden_done")
        xn_lo = sem("xn_lo")
        q_lo = sem("q_lo")
        ctx_lo = sem("ctx_lo")
        zn_lo = [sem("zn_lo0"), sem("zn_lo1")]
        arg_done = sem("arg_done")
        y_done = sem("y_done")
        mv1_done = sem("mv1_done")
        ve1_done = sem("ve1_done")
        mv2_done = sem("mv2_done")
        ve2_done = sem("ve2_done")
        xn_done = sem("xn_done")
        zn_done = sem("zn_done")
        rstd1_done = sem("rstd1_done")
        rstd2_done = sem("rstd2_done")
        xb_done = sem("xb_done")
        probs_ready = sem("probs_ready")
        out_done = sem("out_done")

        freed_by = {F: (arg_done, 2), XT: (xn_lo, 2), Q: (q_lo, 4), O: (y_done, 2), Z0: (zn_lo[0], 1),
                    Z1: (zn_lo[1], 1)}
        Z = [Z0, Z1]

        def wait(eng, semaphore, per_tile, tile, k):
            if tile.exists(TILES):
                eng.wait_ge(semaphore, count(per_tile, tile, k))

        def where(kind, n):
            return ps[:, BANK[kind, n], 0:TOK if kind == Q else D]

        def last_user(t, kind, n):
            k = SEQUENCE.index((kind, n))
            for back in range(1, 3 * len(SEQUENCE)):
                other = SEQUENCE[(k - back) % len(SEQUENCE)]
                tile = t - SHIFT[kind] + (k - back) // len(SEQUENCE) + SHIFT[other[0]]
                if BANK[other] == BANK[kind, n] and tile.exists(TILES):
                    return (*other, tile)
            return None

        def four(name, how):
            return [(name, c, how) for c in range(C)]

        plan = ([("b_cols", 0, "d")] + four("ctx_t", "ad") + four("wk_t", "ad")
                + [("wq_t", 0, "ad"), ("wq_t", 1, "ad"), ("key", 0, "k"), ("wq_t", 2, "ad"),
                   ("key", 1, "k"), ("wq_t", 3, "ad"), ("wv_t", 0, "ad"), ("key", 2, "k"),
                   ("wv_t", 1, "ad"), ("wv_t", 2, "ad"), ("key", 3, "k"), ("wv_t", 3, "ad")]
                + four("w0_t", "ad") + four("val", "d"))
        ATTN = len(plan)
        plan += four("w01_t", "ad") + four("wf", "ad") + four("wo_t", "ad")
        names = [(name, c) for name, c, _ in plan]
        on_act = [how in ("ad", "k") for _, _, how in plan]
        on_dve = [how in ("d", "ad", "k") for _, _, how in plan]
        setup_bank = [m % 8 if m < ATTN else m - ATTN if m < ATTN + C else 2 + m % 3 for m in range(len(plan))]
        TRANSPOSED = ("ctx_t", "wk_t", "wq_t", "wv_t", "w0_t", "wo_t")

        def placed(dst, name, c):
            return dst[:, :, c * P:(c + 1) * P] if name in TRANSPOSED else dst[:, c]

        def in_bank(m):
            bank = ps[:, setup_bank[m]]
            return bank.rearrange("p (k r) -> p k r", k=C) if names[m][0] in TRANSPOSED else bank

        def setup_copied(eng, m):
            if on_act[m]:
                eng.wait_ge(s_act, sum(on_act[:m + 1]))
            if on_dve[m]:
                eng.wait_ge(s_dve, sum(on_dve[:m + 1]))

        def setup_all(eng, name):
            for m in (names.index((name, 2)), names.index((name, 3))):
                setup_copied(eng, m)

        def products(*wanted, chunks=range(C)):
            return [m for m, (name, c) in enumerate(names) if name in wanted and c in chunks]

        AHEAD = 2

        def ahead(t, n):
            return t.i is None and t.s == 0 and n < AHEAD

        def blocks_filled(eng):
            eng.wait_ge(s_blocks, 16 * (C // 2) * HG * 2 * 2)

        block = ctx.enter_context(nc.Block())

        @block.sync
        def _(sp):
            def load_rows(dst, src, landed):
                for r in range(C):
                    sp.dma_start(dst[:, r], src[r * P:(r + 1) * P, :]).then_inc(landed[r], 16)

            def load(t):
                j = t.s // UNROLL if t.i is None else t.i + t.s // UNROLL
                sp.dma_start(x_sb[t.s % UNROLL][:], x_view[t.s % B, j]).then_inc(x_in[t.s % UNROLL], 16)

            load_rows(ctx_nat, ctx_in.rearrange("b s d -> (b s) d"), L_CTX)
            load_rows(wk_nat, w_in[D:2 * D, :], L_WK)
            load_rows(wq_nat, w_in[0:D, :], L_WQ)
            load_rows(wv_nat, w_in[2 * D:3 * D, :], L_WV)
            for t in range(2):
                load(Tile(t))
            load_rows(w0_nat, w_ffn, L_W0)
            load_rows(w1_nat, w_aux1, L_W1)
            load_rows(w2_nat, w_aux2, L_W2)

            sp.wait_ge(zeros, 2)
            for c in range(0, C, 2):
                for k in (c, c + 1):
                    setup_copied(sp, names.index(("key", k)))
                for j in range(HG):
                    h = j % 2
                    for half, kc in ((HI, key_hi), (LO, key_lo)):
                        for row in (HD * h, P // 2 + HD * h):
                            sp.dma_start(
                                keys[row:row + HD, half, j // 2, c:c + 2, :, h * S:(h + 1) * S]
                                .bitcast(F32).rearrange("p c b s -> p (c b) s"),
                                kc[HD * j:HD * (j + 1), c:c + 2, :].rearrange("p c (b s) -> p (c b) s", b=B),
                            ).then_inc(s_blocks, 16)

            sp.wait_ge(s_mm, products("val")[-1] + 1)
            blocks_filled(sp)
            for t in range(2, UNROLL):
                load(Tile(t))
            sp.wait_ge(s_mm, products("w01_t")[-1] + 1)
            load_rows(wo_nat, w_out, L_WO)

            def iteration(t):
                done, more = t - 2, t + 2
                for s in range(SUB):
                    if done.exists(TILES):
                        wait(sp, out_done, 2, done, s)
                        j = done.s // UNROLL if t.i is None else t.i + done.s // UNROLL
                        sp.dma_start(out_view[done.s % B, j, s], work[:, s]).then_inc(stored[s], 16)
                if done.exists(TILES) and more.exists(TILES):
                    load(more)

            for t in PROLOGUE:
                iteration(t)
            with sp.Fori(0, LOOPS) as i:
                for k in range(UNROLL):
                    iteration(Tile(2 + k, i))
            for t in EPILOGUE:
                iteration(t)
            for s in range(SUB):
                sp.wait_ge(stored[s], 16 * TILES)

        @block.gpsimd
        def _(pool):
            nc.gpsimd.memset(ident[:], 0.0).then_inc(consts, 1)
            nc.gpsimd.memset(minus_half[:], -0.5).then_inc(consts, 1)
            pool.wait_ge(consts, 2)
            nc.gpsimd.affine_select(out=ident[:], in_=ident[:], compare_op=ALU.not_equal, fill=1.0, base=0,
                                    pattern=[[-1, P]], channel_multiplier=1).then_inc(consts, 1)
            for h in range(2):
                nc.gpsimd.memset(keys[:, h].bitcast(F32), 0.0).then_inc(zeros, 1)
            pool.wait_ge(L_B, 16 * 2)

            def normalise_probs(t, n, now=False):
                g, s = n // 2, n % 2
                if not t.exists(TILES) or (ahead(t, n) and not now):
                    return
                wait(pool, rden_done, 8, t, n)
                pr = probs[:, g % 2, s].rearrange("p (h k) -> p h k", h=HG)
                nc.gpsimd.tensor_tensor(pr, pr, rden[:, n].unsqueeze(2).to_broadcast([P, HG, S]),
                                        ALU.mult).then_inc(probs_ready, 1)

            def add_bias(t, s):
                if t.exists(TILES):
                    wait(pool, xn_done, 2, t, s)
                    xs = x_sb[t.s % UNROLL][:, s]
                    nc.gpsimd.tensor_tensor(xs, xs, bo_row[:], ALU.add).then_inc(xb_done, 1)

            def result(t, s):
                if t.exists(TILES):
                    wait(pool, tanh_done, 2, t, s)
                    nc.gpsimd.tensor_tensor(work[:, s], work[:, s], x_sb[t.s % UNROLL][:, s],
                                            ALU.add).then_inc(out_done, 1)

            def y_rstd(t, s):
                if t.exists(TILES):
                    wait(pool, ve2_done, 2, t, s)
                    nc.gpsimd.tensor_tensor(rstd2[:, s:s + 1], ve2[:, s:s + 1], minus_half[:, 0:1],
                                            ALU.pow).then_inc(rstd2_done, 1)

            def x_rstd(t):
                if t.exists(TILES):
                    wait(pool, ve1_done, 1, t, 0)
                    nc.gpsimd.tensor_tensor(rstd1[:], ve1[:], minus_half[:], ALU.pow).then_inc(rstd1_done, 1)

            def iteration(t):
                normalise_probs(t, 0)
                normalise_probs(t, 1)
                result(t - 2, 0)
                result(t - 2, 1)
                add_bias(t + 1, 0)
                normalise_probs(t, 2)
                normalise_probs(t, 3)
                normalise_probs(t, 4)
                y_rstd(t - 1, 0)
                x_rstd(t + 2)
                normalise_probs(t, 5)
                normalise_probs(t, 6)
                y_rstd(t - 1, 1)
                add_bias(t + 1, 1)
                normalise_probs(t, 7)

            x_rstd(Tile(0))
            for s in range(SUB):
                add_bias(Tile(0), s)
            x_rstd(Tile(1))
            for n in range(AHEAD):
                normalise_probs(Tile(0), n, now=True)
            for t in PROLOGUE:
                iteration(t)
            with pool.Fori(0, LOOPS) as i:
                for k in range(UNROLL):
                    iteration(Tile(2 + k, i))
            for t in EPILOGUE:
                iteration(t)

        @block.scalar
        def _(act):
            act.dma_start(b_rows[:], b_in[0:2 * D].rearrange("(c p) -> c p", p=P)).then_inc(L_QK, 16)
            act.dma_start(vals[:, B - 1], b_in[2 * D:3 * D].partition_broadcast(P)).then_inc(L_V, 16)
            act.dma_start(bo_row[:], b_out.partition_broadcast(P)).then_inc(L_B, 16)
            act.dma_start(bf_row[:], b_ffn.partition_broadcast(P)).then_inc(L_B, 16)

            def setup_copy(*names_wanted, chunks=range(C)):
                for m in products(*names_wanted, chunks=chunks):
                    name, c, how = plan[m]
                    if not on_act[m]:
                        continue
                    act.wait_ge(s_mm, m + 1)
                    if name == "key":
                        act.wait_ge(s_key, c + 1)
                    nc.scalar.copy(placed(split[name][HI], name, c), in_bank(m)).then_inc(s_act, 1)

            def setup_split(name, nat, landed):
                for c in range(C):
                    act.wait_ge(landed[c], 16)
                    nc.scalar.copy(split[name][HI][:, c], nat[:, c]).then_inc(s_split_hi, 1)

            def exps(t, n, now=False):
                g, s = n // 2, n % 2
                if not t.exists(TILES) or (ahead(t, n) and not now):
                    return
                wait(act, max_done, 8, t, n)
                wait(act, pt_ready, 8, t if g >= 2 else t - 1, 2 * g - 3 if g >= 2 else 2 * g + 5)
                for h in range(HG):
                    last = nc.scalar.activation(probs[:, g % 2, s, h * S:(h + 1) * S],
                                                ps[:, n % 2, h * S:(h + 1) * S], ACT.Exp,
                                                bias=neg_max[:, n, h:h + 1], accum_out=den[:, n, h:h + 1])
                last.then_inc(exp_done, 1)

            def copy_probs_t(t, idx):
                g = idx // 2
                if t.exists(TILES):
                    wait(act, pt_ready, 8, t, idx)
                    wait(act, ctx_ready, 4, t if g >= 2 else t - 1, (g - 2) % 4)
                    nc.scalar.copy(probs_t[:, g % 2, 2:4].rearrange("p h t -> p (h t)"),
                                   ps[:, 2 + idx % 2]).then_inc(pt_act, 1)

            def context_hi(t, g):
                if t.exists(TILES):
                    wait(act, ctx_ready, 4, t, g)
                    wait(act, dense_ready[O], 2, t - 2, 1)
                    nc.scalar.copy(ctx_o[HI][:, t.s % 2, g], ps[:, CTX_BANK, 0:TOK]).then_inc(ctx_hi, 1)

            def xn_t_hi(t, s):
                if t.exists(TILES):
                    wait(act, dense_ready[XT], 2, t, s)
                    wait(act, dense_ready[Q], 4, t - 1, C - 1)
                    nc.scalar.copy(xn_t[HI][:, :, s * P:(s + 1) * P],
                                   where(XT, s).rearrange("p (c t) -> p c t", c=C)).then_inc(xn_hi, 1)

            def query_hi(t, c):
                if t.exists(TILES):
                    wait(act, dense_ready[Q], 4, t, c)
                    wait(act, scores_ready, 8, t - 1, 2 * c + 1)
                    for pair in range(2):
                        rows = slice(pair * P // 2, (pair + 1) * P // 2)
                        last = nc.scalar.activation(q_st[rows, c, pair], where(Q, c)[rows],
                                                    ACT.Identity, bias=bq_col[rows, c:c + 1])
                    last.then_inc(q_hi, 1)

            def z_t_hi(t, s):
                if t.exists(TILES):
                    wait(act, dense_ready[Z[s]], 1, t, 0)
                    wait(act, dense_ready[F], 2, t - 1, s)
                    nc.scalar.copy(zn_t[HI][:, s].rearrange("p c t -> p (c t)"),
                                   where(Z[s], 0)).then_inc(zn_hi[s], 1)

            def tanh(t, s):
                if t.exists(TILES):
                    wait(act, arg_done, 2, t, s)
                    nc.scalar.activation(work[:, s], work[:, s], ACT.Tanh).then_inc(tanh_done, 1)

            def iteration(t):
                query_hi(t, 3)
                z_t_hi(t - 2, 1)
                context_hi(t - 1, 2)
                exps(t, 0)
                exps(t, 1)
                copy_probs_t(t - 1, 7)
                tanh(t - 2, 0)
                xn_t_hi(t + 1, 0)
                xn_t_hi(t + 1, 1)
                exps(t, 2)
                context_hi(t - 1, 3)
                tanh(t - 2, 1)
                exps(t, 3)
                query_hi(t + 1, 0)
                copy_probs_t(t, 1)
                exps(t, 4)
                context_hi(t, 0)
                copy_probs_t(t, 3)
                exps(t, 5)
                query_hi(t + 1, 1)
                context_hi(t, 1)
                exps(t, 6)
                z_t_hi(t - 1, 0)
                query_hi(t + 1, 2)
                exps(t, 7)
                copy_probs_t(t, 5)

            setup_copy("ctx_t", "wk_t", "key", "wq_t", "wv_t", "w0_t")
            setup_split("w1", w1_nat, L_W1)
            setup_split("w2", w2_nat, L_W2)
            setup_copy("w01_t", chunks=range(2))
            xn_t_hi(Tile(0), 0)
            setup_copy("w01_t", chunks=[2])
            xn_t_hi(Tile(0), 1)
            setup_copy("w01_t", chunks=[3])
            blocks_filled(act)
            for c in range(2):
                query_hi(Tile(0), c)
                setup_copy("wf", chunks=[c])
            for n in range(AHEAD):
                exps(Tile(0), n, now=True)
            query_hi(Tile(0), 2)
            setup_copy("wf", chunks=range(2, C))
            setup_copy("wo_t")
            for t in PROLOGUE:
                iteration(t)
            with act.Fori(0, LOOPS) as i:
                for k in range(UNROLL):
                    iteration(Tile(2 + k, i))
            for t in EPILOGUE:
                iteration(t)

        @block.vector
        def _(dve):
            dve.wait_ge(L_V, 16)
            dve.wait_ge(L_B, 16 * 2)

            def setup_copy(*names_wanted, chunks=range(C)):
                for m in products(*names_wanted, chunks=chunks):
                    name, c, how = plan[m]
                    if not on_dve[m]:
                        continue
                    dve.wait_ge(s_mm, m + 1)
                    bank = in_bank(m)
                    if name == "key":
                        nc.vector.tensor_scalar(bank, bank, bk_col[:, c:c + 1], SCALE,
                                                ALU.add, ALU.mult).then_inc(s_key, 1)
                        dve.wait_ge(s_key, c + 1)
                    if how in ("ad", "k"):
                        dve.wait_ge(s_act, sum(on_act[:m + 1]))
                        hi, lo = (placed(half, name, c) for half in split[name])
                        nc.vector.tensor_tensor(lo, bank, hi.bitcast(F32), ALU.subtract).then_inc(s_dve, 1)
                    elif name == "val":
                        nc.vector.tensor_tensor(vals[:, c], bank, vals[:, B - 1], ALU.add).then_inc(s_dve, 1)
                    else:
                        nc.vector.tensor_copy(b_cols[:], bank[:, 0:2 * C]).then_inc(s_dve, 1)
                        dve.wait_ge(s_dve, 1)

            def setup_split(name, nat, done):
                for c in range(C):
                    dve.wait_ge(s_split_hi, done + c + 1)
                    nc.vector.tensor_tensor(split[name][LO][:, c], nat[:, c], split[name][HI][:, c].bitcast(F32),
                                            ALU.subtract).then_inc(s_split_lo, 1)

            def maxima(t, n, now=False):
                if not t.exists(TILES) or (ahead(t, n) and not now):
                    return
                wait(dve, scores_ready, 8, t, n)
                nc.vector.tensor_reduce(neg_max[:, n], ps[:, n % 2].rearrange("p (h k) -> p h k", h=HG),
                                        AX.X, ALU.max, negate=True).then_inc(max_done, 1)

            def reciprocals(t, n, now=False):
                if not t.exists(TILES) or (ahead(t, n) and not now):
                    return
                wait(dve, exp_done, 8, t, n)
                nc.vector.reciprocal(rden[:, n], den[:, n]).then_inc(rden_done, 1)

            def copy_probs_t(t, idx):
                g = idx // 2
                if t.exists(TILES):
                    wait(dve, pt_ready, 8, t, idx)
                    wait(dve, ctx_ready, 4, t if g >= 2 else t - 1, (g - 2) % 4)
                    nc.vector.tensor_copy(probs_t[:, g % 2, 0:2].rearrange("p h t -> p (h t)"),
                                          ps[:, 2 + idx % 2]).then_inc(pt_dve, 1)

            def context_lo(t, g):
                if t.exists(TILES):
                    wait(dve, ctx_hi, 4, t, g)
                    nc.vector.tensor_tensor(ctx_o[LO][:, t.s % 2, g], ps[:, CTX_BANK, 0:TOK],
                                            ctx_o[HI][:, t.s % 2, g].bitcast(F32), ALU.subtract).then_inc(ctx_lo, 1)

            def xn_t_lo(t, s):
                if t.exists(TILES):
                    wait(dve, xn_hi, 2, t, s)
                    cols = slice(s * P, (s + 1) * P)
                    nc.vector.tensor_tensor(xn_t[LO][:, :, cols],
                                            where(XT, s).rearrange("p (c t) -> p c t", c=C),
                                            xn_t[HI][:, :, cols].bitcast(F32), ALU.subtract).then_inc(xn_lo, 1)

            def query_lo(t, c):
                if t.exists(TILES):
                    wait(dve, q_hi, 4, t, c)
                    for pair in range(2):
                        rows = slice(pair * P // 2, (pair + 1) * P // 2)
                        other = slice((1 - pair) * P // 2, (2 - pair) * P // 2)
                        last = nc.vector.scalar_tensor_tensor(
                            out=q_st[other, c, pair], in0=where(Q, c)[rows],
                            scalar=bq_col[rows, c:c + 1], in1=q_st[rows, c, pair].bitcast(F32),
                            op0=ALU.add, op1=ALU.subtract)
                    last.then_inc(q_lo, 1)

            def z_t_lo(t, s):
                if t.exists(TILES):
                    wait(dve, zn_hi[s], 1, t, 0)
                    nc.vector.tensor_tensor(zn_t[LO][:, s].rearrange("p c t -> p (c t)"), where(Z[s], 0),
                                            zn_t[HI][:, s].rearrange("p c t -> p (c t)").bitcast(F32),
                                            ALU.subtract).then_inc(zn_lo[s], 1)

            def tanh_argument(t, s):
                if t.exists(TILES):
                    wait(dve, dense_ready[F], 2, t, s)
                    nc.vector.tensor_tensor(work[:, s], where(F, s), bf_row[:], ALU.add).then_inc(arg_done, 1)

            def x_statistics(t):
                if t.exists(TILES):
                    slot = t.s % UNROLL
                    turns = t.s // UNROLL + 1 if t.i is None else t.i + (t.s // UNROLL + 1)
                    dve.wait_ge(x_in[slot], turns * 16)
                    wait(dve, rstd1_done, 1, t - 1, 0)
                    for s in range(SUB):
                        nc.vector.bn_stats(st1[:, s], x_sb[slot][:, s])
                    nc.vector.drain()
                    for s in range(SUB):
                        nc.vector.bn_aggr(mv1[:, s], st1[:, s]).then_inc(mv1_done, 1)
                    wait(dve, mv1_done, 2, t, 1)
                    nc.vector.tensor_scalar_add(ve1[:], mv1[:, :, 1], EPS).then_inc(ve1_done, 1)

            def x_normalise(t, s):
                if t.exists(TILES):
                    wait(dve, rstd1_done, 1, t, 0)
                    wait(dve, dense_ready[XT], 2, t - 1, s)
                    nc.vector.tensor_scalar(xn[:, s], x_sb[t.s % UNROLL][:, s], mv1[:, s, 0:1],
                                            rstd1[:, s:s + 1], ALU.subtract, ALU.mult).then_inc(xn_done, 1)

            def residual(t, s):
                if t.exists(TILES):
                    xs = x_sb[t.s % UNROLL][:, s]
                    wait(dve, dense_ready[O], 2, t, s)
                    wait(dve, xb_done, 2, t, s)
                    nc.vector.tensor_tensor(xs, where(O, s), xs, ALU.add).then_inc(y_done, 1)
                    wait(dve, y_done, 2, t, s)
                    nc.vector.bn_stats(st2[:, s], xs)

            def y_statistics(t, s):
                if t.exists(TILES):
                    nc.vector.drain()
                    nc.vector.bn_aggr(mv2[:, s], st2[:, s]).then_inc(mv2_done, 1)
                    wait(dve, mv2_done, 2, t, s)
                    nc.vector.tensor_scalar_add(ve2[:, s:s + 1], mv2[:, s, 1:2], EPS).then_inc(ve2_done, 1)

            def y_normalise(t, s):
                if t.exists(TILES):
                    wait(dve, rstd2_done, 2, t, s)
                    if (t - 1).exists(TILES):
                        dve.wait_ge(stored[s], 16 * t.s if t.i is None else t.i * (16 * UNROLL) + 16 * t.s)
                    nc.vector.tensor_scalar(work[:, s], x_sb[t.s % UNROLL][:, s], mv2[:, s, 0:1],
                                            rstd2[:, s:s + 1], ALU.subtract, ALU.mult).then_inc(zn_done, 1)

            def iteration(t):
                query_lo(t, 3)
                maxima(t, 0)
                z_t_lo(t - 2, 1)
                maxima(t, 1)
                context_lo(t - 1, 2)
                tanh_argument(t - 2, 0)
                reciprocals(t, 0)
                maxima(t, 2)
                reciprocals(t, 1)
                copy_probs_t(t - 1, 6)
                xn_t_lo(t + 1, 0)
                xn_t_lo(t + 1, 1)
                tanh_argument(t - 2, 1)
                context_lo(t - 1, 3)
                copy_probs_t(t, 0)
                maxima(t, 3)
                reciprocals(t, 2)
                maxima(t, 4)
                reciprocals(t, 3)
                query_lo(t + 1, 0)
                residual(t - 1, 0)
                copy_probs_t(t, 2)
                maxima(t, 5)
                y_statistics(t - 1, 0)
                reciprocals(t, 4)
                context_lo(t, 0)
                x_statistics(t + 2)
                reciprocals(t, 5)
                maxima(t, 6)
                query_lo(t + 1, 1)
                y_normalise(t - 1, 0)
                x_normalise(t + 2, 0)
                context_lo(t, 1)
                residual(t - 1, 1)
                reciprocals(t, 6)
                maxima(t, 7)
                z_t_lo(t - 1, 0)
                y_statistics(t - 1, 1)
                copy_probs_t(t, 4)
                reciprocals(t, 7)
                y_normalise(t - 1, 1)
                query_lo(t + 1, 2)
                x_normalise(t + 2, 1)

            setup_copy("b_cols", "ctx_t", "wk_t", "key", "wq_t", "wv_t", "w0_t")
            x_statistics(Tile(0))
            setup_split("w1", w1_nat, 0)
            setup_copy("val")
            for s in range(SUB):
                x_normalise(Tile(0), s)
            setup_split("w2", w2_nat, C)
            setup_copy("w01_t", chunks=range(2))
            xn_t_lo(Tile(0), 0)
            setup_copy("w01_t", chunks=[2])
            xn_t_lo(Tile(0), 1)
            setup_copy("w01_t", chunks=[3])
            x_statistics(Tile(1))
            for c in range(2):
                query_lo(Tile(0), c)
                setup_copy("wf", chunks=[c])
            for n in range(AHEAD):
                maxima(Tile(0), n, now=True)
            for n in range(AHEAD):
                reciprocals(Tile(0), n, now=True)
            query_lo(Tile(0), 2)
            for s in range(SUB):
                x_normalise(Tile(1), s)
            setup_copy("wf", chunks=range(2, C))
            setup_copy("wo_t")
            for t in PROLOGUE:
                iteration(t)
            with dve.Fori(0, LOOPS) as i:
                for k in range(UNROLL):
                    iteration(Tile(2 + k, i))
            for t in EPILOGUE:
                iteration(t)

        @block.tensor
        def _(pe):
            pe.wait_ge(consts, 3)
            nat = {"ctx_t": (ctx_nat, L_CTX), "wk_t": (wk_nat, L_WK), "wq_t": (wq_nat, L_WQ),
                   "wv_t": (wv_nat, L_WV), "w0_t": (w0_nat, L_W0), "wo_t": (wo_nat, L_WO)}

            PASSES = [(half, k) for half in ((HI, HI), (LO, HI), (HI, LO)) for k in range(C)]

            def product(bank, lhs_t, cols, rhs):
                for j, ((a, b), k) in enumerate(PASSES):
                    last = nc.tensor.matmul(bank, split[lhs_t][a][:, k, cols], split[rhs][b][:, k],
                                            start=(j == 0), stop=(j == len(PASSES) - 1))
                return last

            def setup_products(*names_wanted, chunks=range(C)):
                for m in products(*names_wanted, chunks=chunks):
                    last = setup_product(m)
                    last.then_inc(s_mm, 1)

            def setup_product(m):
                name, c, how = plan[m]
                bank = ps[:, setup_bank[m]]
                if setup_bank[m] in setup_bank[:m]:
                    setup_copied(pe, max(k for k in range(m) if setup_bank[k] == setup_bank[m]))
                cols = slice(c * P, (c + 1) * P)
                if name == "b_cols":
                    pe.wait_ge(L_QK, 16)
                    return nc.tensor.transpose(bank[:, 0:2 * C], b_rows[:], ident[0:2 * C, 0:2 * C])
                if name in nat:
                    src, landed = nat[name]
                    pe.wait_ge(landed[c], 16)
                    for k in range(C):
                        last = nc.tensor.transpose(bank[:, k * P:(k + 1) * P], src[:, c, k * P:(k + 1) * P], ident[:])
                    return last
                if name == "key":
                    if c == 0:
                        setup_all(pe, "ctx_t")
                        setup_all(pe, "wk_t")
                    return product(bank, "wk_t", cols, "ctx_t")
                if name == "val":
                    if c == 0:
                        setup_all(pe, "wv_t")
                    return product(bank, "ctx_t", cols, "wv_t")
                if name == "w01_t":
                    if c == 0:
                        pe.wait_ge(s_split_lo, C)
                        setup_all(pe, "w0_t")
                    return product(bank, "w1", cols, "w0_t")
                if c == 0:
                    pe.wait_ge(s_split_lo, 2 * C)
                    setup_all(pe, "w01_t")
                return product(bank, "w01_t", cols, "w2")

            def scores(t, n, now=False):
                g, s = n // 2, n % 2
                if not t.exists(TILES) or (ahead(t, n) and not now):
                    return
                wait(pe, q_lo, 4, t, g)
                wait(pe, exp_done, 8, t if n >= 2 else t - 1, (n - 2) % 8)
                for pair in range(2):
                    for half in (HI, LO):
                        last = nc.tensor.matmul(ps[:, n % 2, pair * 2 * S:(pair + 1) * 2 * S],
                                                q_st[:, g, pair, s * P:(s + 1) * P],
                                                keys[:, half, pair, g, t.s % B],
                                                start=(half == HI), stop=(half == LO))
                last.then_inc(scores_ready, 1)

            def transpose_probs(t, idx):
                if not t.exists(TILES):
                    return
                g, pair = idx // 2, idx % 2
                if t.i is None and t.s == 0 and idx == 0:
                    setup_copied(pe, len(plan) - 1)
                wait(pe, probs_ready, 8, t, 2 * g + 1)
                wait(pe, pt_dve if idx % 2 == 0 else pt_act, 4, t if g else t - 1, (g - 1) % 4)
                for h in range(2):
                    for s in range(SUB):
                        col = (2 * pair + h) * S
                        last = nc.tensor.transpose(ps[:, 2 + idx % 2, (h * SUB + s) * P:(h * SUB + s + 1) * P],
                                                   probs[:, g % 2, s, col:col + S], ident[:])
                last.then_inc(pt_ready, 1)

            def context(t, g):
                if not t.exists(TILES):
                    return
                wait(pe, pt_dve, 4, t, g)
                wait(pe, pt_act, 4, t, g)
                wait(pe, ctx_lo, 4, t if g else t - 1, (g - 1) % 4)
                for h in range(HG):
                    f = (g * HG + h) * HD
                    last = nc.tensor.matmul(ps[HD * h:HD * (h + 1), CTX_BANK, 0:TOK],
                                            vals[:, t.s % B, f:f + HD], probs_t[:, g % 2, h],
                                            start=True, stop=True, tile_position=(0, HD * h))
                last.then_inc(ctx_ready, 1)

            def dense(t, kind, n, start=0, end=None):
                end = end or PARTS[kind]
                if not t.exists(TILES):
                    return
                dst = where(kind, n)
                if start == 0:
                    before = last_user(t, kind, n)
                    if before:
                        freed, per_tile = freed_by[before[0]]
                        wait(pe, freed, per_tile, before[2], before[1])
                if kind in (XT, Z0, Z1):
                    half = {XT: n, Z0: 0, Z1: 1}[kind]
                    src, ready = (xn, xn_done) if kind == XT else (work, zn_done)
                    wait(pe, ready, 2, t, half)
                    for c in range(C):
                        last = nc.tensor.transpose(dst[:, c * P:(c + 1) * P], src[:, half, c * P:(c + 1) * P], ident[:])
                    last.then_inc(dense_ready[kind], 1)
                    return
                if kind == Q:
                    if start == 0:
                        wait(pe, xn_lo, 2, t, 1)
                elif kind == O:
                    if start == 0:
                        wait(pe, ctx_lo, 4, t, C - 1)
                else:
                    if start == 0:
                        wait(pe, zn_lo[n], 1, t, 0)
                size = len(PASSES) // PARTS[kind]
                for j in range(start * size, end * size):
                    (a, w), k = PASSES[j]
                    if kind == Q:
                        lhs, rhs = wq[w][:, k, n * P:(n + 1) * P], xn_t[a][:, k]
                    elif kind == O:
                        lhs, rhs = ctx_o[a][:, t.s % 2, k, n * P:(n + 1) * P], wo[w][:, k]
                    else:
                        lhs, rhs = zn_t[a][:, n, k], wf[w][:, k]
                    last = nc.tensor.matmul(dst, lhs, rhs, start=(j == 0), stop=(j == len(PASSES) - 1))
                if end == PARTS[kind]:
                    last.then_inc(dense_ready[kind], 1)

            def iteration(t):
                scores(t, 0)
                transpose_probs(t - 1, 5)
                dense(t - 2, F, 0, 0, 2)
                context(t - 1, 2)
                dense(t - 2, Z1, 0)
                scores(t, 1)
                transpose_probs(t - 1, 6)
                transpose_probs(t - 1, 7)
                dense(t - 2, F, 0, 2, 4)
                dense(t - 2, F, 1, 0, 1)
                scores(t, 2)
                dense(t + 1, XT, 0)
                dense(t + 1, XT, 1)
                dense(t - 2, F, 1, 1, 4)
                context(t - 1, 3)
                transpose_probs(t, 0)
                dense(t + 1, Q, 0, 0, 1)
                scores(t, 3)
                dense(t - 1, O, 0, 0, 1)
                scores(t, 4)
                transpose_probs(t, 1)
                dense(t + 1, Q, 0, 1, 2)
                dense(t - 1, O, 0, 1, 4)
                context(t, 0)
                transpose_probs(t, 2)
                scores(t, 5)
                dense(t + 1, Q, 1, 0, 1)
                transpose_probs(t, 3)
                dense(t + 1, Q, 1, 1, 2)
                scores(t, 6)
                dense(t - 1, O, 1, 0, 3)
                context(t, 1)
                scores(t, 7)
                dense(t - 1, O, 1, 3, 4)
                dense(t + 1, Q, 2, 0, 1)
                dense(t - 1, Z0, 0)
                dense(t + 1, Q, 2, 1, 2)
                dense(t + 1, Q, 3)
                transpose_probs(t, 4)

            setup_products("b_cols", "ctx_t", "wk_t", "key", "wq_t", "wv_t", "w0_t", "val")
            setup_products("w01_t", chunks=range(2))
            setup_copied(pe, ATTN - 1)
            dense(Tile(0), XT, 0)
            setup_products("w01_t", chunks=[2])
            dense(Tile(0), XT, 1)
            setup_products("w01_t", chunks=[3])
            for c in range(2):
                dense(Tile(0), Q, c)
                setup_products("wf", chunks=[c])
            blocks_filled(pe)
            for n in range(AHEAD):
                scores(Tile(0), n, now=True)
            dense(Tile(0), Q, 2)
            setup_products("wf", chunks=range(2, C))
            setup_products("wo_t")
            dense(Tile(0), Q, 3)
            for t in PROLOGUE:
                iteration(t)
            with pe.Fori(0, LOOPS) as i:
                for k in range(UNROLL):
                    iteration(Tile(2 + k, i))
            for t in EPILOGUE:
                iteration(t)


_INS = ["x", "ctx_1024", "L0_xattn_in_proj_weight", "L0_xattn_in_proj_bias", "L0_xattn_out_w", "L0_xattn_out_b",
        "L0_ffn_weight", "L0_ffn_aux_weight1", "L0_ffn_aux_weight2", "L0_ffn_bias"]


def kernel(**inputs):
    import numpy as _np
    import concourse.bacc as _bacc
    from concourse import mybir as _mybir
    from concourse.bass_utils import run_bass_kernel_spmd as _run

    nc = _bacc.Bacc("TRN2", target_bir_lowering=False, num_devices=1)
    arrays, args = {}, []
    for name in _INS:
        a = _np.ascontiguousarray(inputs[name])
        arrays[f"in_{name}"] = a
        args.append(nc.dram_tensor(f"in_{name}", a.shape, _mybir.dt.from_np(a.dtype), kind="ExternalInput").ap())
    shape = inputs["x"].shape
    args.append(nc.dram_tensor("out_y", shape, _mybir.dt.float32, kind="ExternalOutput").ap())
    build(nc, *args)
    r = _run(nc, [arrays], core_ids=[0])
    return r.results[0]["out_y"]
```
